# Optimizing a Trainium2 kernel written in Bass

```python
import numpy as np
import jax
import jax.numpy as jnp

def _softmax(x, axis=-1):
    return jax.nn.softmax(x, axis=axis)

def _gelu(x):
    return jax.nn.gelu(x, approximate=True)

def _silu(x):
    return jax.nn.silu(x)

def _sigmoid(x):
    return jax.nn.sigmoid(x)

def _layernorm(x, axis=-1, eps=1e-05):
    m = jnp.mean(x, axis=axis, keepdims=True)
    v = jnp.var(x, axis=axis, keepdims=True)
    return (x - m) / jnp.sqrt(v + eps)

def _scatter_add(tgt, idx, src, axis=0):
    return tgt.at[idx].add(src)

def _segment_sum(src, seg, n):
    return jax.ops.segment_sum(src, seg, n)
kernel_name = 'mk_audio_tower_d1_tok_audfeat512_r4_32d3b5'

def setup_inputs(seed: int=0):
    np.random.seed(seed)
    _w = jnp.asarray

    def _rec_inputs():
        import jax
        import jax.numpy as jnp
        _rk = jax.random.key(seed)
        x = -7.10856e-05 + 0.999911 * jax.random.normal(jax.random.fold_in(_rk, 1), (128, 256, 128), jnp.float32)
        return x
    x = _rec_inputs()

    def _L0_tok_setup():
        import jax, jax.numpy as jnp
        import numpy as np
        BLOCK = 128
        TOP_K = 16
        key = jax.random.key(seed)
        k1, k2 = jax.random.split(key)
        B, S, D = (8, 4096, 128)
        x = jax.random.normal(k1, (B, S, D), dtype=jnp.float32)
        W = jax.random.normal(k2, (1, D), dtype=jnp.float32) * (1.0 / np.sqrt(D))
        b = jnp.zeros((1,), dtype=jnp.float32)
        return {'x': x, 'W': W, 'b': b}
    _L0_tok_all = _L0_tok_setup()
    _L0_tok_in = {k: v for k, v in _L0_tok_all.items() if k in ('W', 'b')}
    del _L0_tok_all

    def _L0_attn_setup():
        import jax, jax.numpy as jnp
        import numpy as np
        SIZE = 128
        NUM_HEADS = 8
        HEAD_SIZE = SIZE // NUM_HEADS
        EPS = 1e-05

        def _retention(x, W_Q, W_K, W_V):
            B, T, D = x.shape
            H, dh = (NUM_HEADS, HEAD_SIZE)
            q = (x @ W_Q).reshape(B, T, H, dh).transpose(0, 2, 1, 3)
            k = (x @ W_K).reshape(B, T, H, dh).transpose(0, 2, 1, 3)
            v = (x @ W_V).reshape(B, T, H, dh).transpose(0, 2, 1, 3)
            gammas = 1.0 - jnp.exp2(-5.0 - jnp.arange(H, dtype=jnp.float32))
            idx = jnp.arange(T)
            diff = (idx[:, None] - idx[None, :]).astype(jnp.float32)
            causal = diff >= 0
            decay = jnp.where(causal[None], jnp.exp(diff[None] * jnp.log(gammas)[:, None, None]), 0.0)
            scores = jnp.einsum('bhtd,bhsd->bhts', q, k) / jnp.sqrt(jnp.float32(dh))
            out = jnp.einsum('bhts,bhsd->bhtd', scores * decay[None], v)
            return out.transpose(0, 2, 1, 3).reshape(B, T, D)

        def _group_norm(y, weight, bias):
            B, T, D = y.shape
            g = y.reshape(B * T, NUM_HEADS, HEAD_SIZE)
            mean = jnp.mean(g, axis=-1, keepdims=True)
            var = jnp.var(g, axis=-1, keepdims=True)
            g = (g - mean) / jnp.sqrt(var + EPS)
            g = g.reshape(B * T, D) * weight + bias
            return g.reshape(B, T, D)
        key = jax.random.key(seed)
        ks = jax.random.split(key, 8)
        B, T, D = (2, 512, SIZE)
        mk = lambda k: jax.random.normal(k, (D, D), dtype=jnp.float32) / D
        return {'x': jax.random.normal(ks[0], (B, T, D), dtype=jnp.float32), 'W_Q': mk(ks[1]), 'W_K': mk(ks[2]), 'W_V': mk(ks[3]), 'W_G': mk(ks[4]), 'W_O': mk(ks[5]), 'gn_weight': jnp.ones((D,), dtype=jnp.float32), 'gn_bias': jnp.zeros((D,), dtype=jnp.float32)}
    _L0_attn_all = _L0_attn_setup()
    _L0_attn_in = {k: v for k, v in _L0_attn_all.items() if k in ('W_Q', 'W_K', 'W_V', 'W_G', 'W_O', 'gn_weight', 'gn_bias')}
    del _L0_attn_all

    def _L0_ffn_setup():
        import jax, jax.numpy as jnp
        import numpy as np
        EPS = 1e-05
        TOP_K = 2

        def layer_norm(x, g, b):
            m = x.mean(-1, keepdims=True)
            v = ((x - m) ** 2).mean(-1, keepdims=True)
            return (x - m) / jnp.sqrt(v + EPS) * g + b
        key = jax.random.key(seed)
        ks = jax.random.split(key, 8)
        B, S, D, E, H = (8, 128, 128, 8, 512)
        x = jax.random.normal(ks[0], (B, S, D), dtype=jnp.float32)
        Wg = jax.random.normal(ks[1], (D, E), dtype=jnp.float32) * 0.02
        W1 = jax.random.normal(ks[2], (E, D, H), dtype=jnp.float32) * 0.02
        b1 = jnp.zeros((E, H), dtype=jnp.float32)
        W2 = jax.random.normal(ks[3], (E, H, D), dtype=jnp.float32) * 0.02
        b2 = jnp.zeros((E, D), dtype=jnp.float32)
        ln_g = jnp.ones((D,), dtype=jnp.float32)
        ln_b = jnp.zeros((D,), dtype=jnp.float32)
        out_g = jnp.ones((D,), dtype=jnp.float32)
        out_b = jnp.zeros((D,), dtype=jnp.float32)
        return {'x': x, 'Wg': Wg, 'W1': W1, 'b1': b1, 'W2': W2, 'b2': b2, 'ln_g': ln_g, 'ln_b': ln_b, 'out_g': out_g, 'out_b': out_b}
    _L0_ffn_all = _L0_ffn_setup()
    _L0_ffn_in = {k: v for k, v in _L0_ffn_all.items() if k in ('Wg', 'W1', 'b1', 'W2', 'b2', 'ln_g', 'ln_b', 'out_g', 'out_b')}
    del _L0_ffn_all
    return {'x': x, 'L0_tok_W': _L0_tok_in['W'], 'L0_tok_b': _L0_tok_in['b'], 'L0_attn_W_Q': _L0_attn_in['W_Q'], 'L0_attn_W_K': _L0_attn_in['W_K'], 'L0_attn_W_V': _L0_attn_in['W_V'], 'L0_attn_W_G': _L0_attn_in['W_G'], 'L0_attn_W_O': _L0_attn_in['W_O'], 'L0_attn_gn_weight': _L0_attn_in['gn_weight'], 'L0_attn_gn_bias': _L0_attn_in['gn_bias'], 'L0_ffn_Wg': _L0_ffn_in['Wg'], 'L0_ffn_W1': _L0_ffn_in['W1'], 'L0_ffn_b1': _L0_ffn_in['b1'], 'L0_ffn_W2': _L0_ffn_in['W2'], 'L0_ffn_b2': _L0_ffn_in['b2'], 'L0_ffn_ln_g': _L0_ffn_in['ln_g'], 'L0_ffn_ln_b': _L0_ffn_in['ln_b'], 'L0_ffn_out_g': _L0_ffn_in['out_g'], 'L0_ffn_out_b': _L0_ffn_in['out_b']}

def reference(x, L0_tok_W, L0_tok_b, L0_attn_W_Q, L0_attn_W_K, L0_attn_W_V, L0_attn_W_G, L0_attn_W_O, L0_attn_gn_weight, L0_attn_gn_bias, L0_ffn_Wg, L0_ffn_W1, L0_ffn_b1, L0_ffn_W2, L0_ffn_b2, L0_ffn_ln_g, L0_ffn_ln_b, L0_ffn_out_g, L0_ffn_out_b):
    import jax
    import jax.numpy as jnp

    def _L0_tok_ref(x, W, b):
        import jax, jax.numpy as jnp
        import numpy as np
        BLOCK = 128
        TOP_K = 16
        B, S, D = x.shape
        n_blocks = S // BLOCK
        scores = jnp.einsum('bsd,d->bs', x, W[0]) + b[0]
        block_scores = scores.reshape(B, n_blocks, BLOCK)
        _, top_idx = jax.lax.top_k(block_scores, TOP_K)
        offsets = (jnp.arange(n_blocks, dtype=top_idx.dtype) * BLOCK)[None, :, None]
        sel_idx = (top_idx + offsets).reshape(B, n_blocks * TOP_K)
        selected_tokens = jnp.take_along_axis(x, sel_idx[:, :, None], axis=1)
        return selected_tokens

    def _L0_attn_ref(x, W_Q, W_K, W_V, W_G, W_O, gn_weight, gn_bias):
        import jax, jax.numpy as jnp
        import numpy as np
        SIZE = 128
        NUM_HEADS = 8
        HEAD_SIZE = SIZE // NUM_HEADS
        EPS = 1e-05

        def _retention(x, W_Q, W_K, W_V):
            B, T, D = x.shape
            H, dh = (NUM_HEADS, HEAD_SIZE)
            q = (x @ W_Q).reshape(B, T, H, dh).transpose(0, 2, 1, 3)
            k = (x @ W_K).reshape(B, T, H, dh).transpose(0, 2, 1, 3)
            v = (x @ W_V).reshape(B, T, H, dh).transpose(0, 2, 1, 3)
            gammas = 1.0 - jnp.exp2(-5.0 - jnp.arange(H, dtype=jnp.float32))
            idx = jnp.arange(T)
            diff = (idx[:, None] - idx[None, :]).astype(jnp.float32)
            causal = diff >= 0
            decay = jnp.where(causal[None], jnp.exp(diff[None] * jnp.log(gammas)[:, None, None]), 0.0)
            scores = jnp.einsum('bhtd,bhsd->bhts', q, k) / jnp.sqrt(jnp.float32(dh))
            out = jnp.einsum('bhts,bhsd->bhtd', scores * decay[None], v)
            return out.transpose(0, 2, 1, 3).reshape(B, T, D)

        def _group_norm(y, weight, bias):
            B, T, D = y.shape
            g = y.reshape(B * T, NUM_HEADS, HEAD_SIZE)
            mean = jnp.mean(g, axis=-1, keepdims=True)
            var = jnp.var(g, axis=-1, keepdims=True)
            g = (g - mean) / jnp.sqrt(var + EPS)
            g = g.reshape(B * T, D) * weight + bias
            return g.reshape(B, T, D)
        ret = _retention(x, W_Q, W_K, W_V)
        normed = _group_norm(ret, gn_weight, gn_bias)
        return jax.nn.silu(x @ W_G + normed) @ W_O

    def _L0_ffn_ref(x, Wg, W1, b1, W2, b2, ln_g, ln_b, out_g, out_b):
        import jax, jax.numpy as jnp
        import numpy as np
        EPS = 1e-05
        TOP_K = 2

        def layer_norm(x, g, b):
            m = x.mean(-1, keepdims=True)
            v = ((x - m) ** 2).mean(-1, keepdims=True)
            return (x - m) / jnp.sqrt(v + EPS) * g + b
        xn = layer_norm(x, ln_g, ln_b)
        logits = jnp.einsum('bsd,de->bse', xn, Wg)
        probs = jax.nn.softmax(logits, axis=-1)
        top_p, top_i = jax.lax.top_k(probs, TOP_K)
        conf = top_p / top_p.sum(-1, keepdims=True)
        h = jax.nn.gelu(jnp.einsum('bsd,edh->bseh', xn, W1) + b1)
        o = jnp.einsum('bseh,ehd->bsed', h, W2) + b2
        sel = jnp.take_along_axis(o, top_i[..., None], axis=2)
        combined = jnp.einsum('bskd,bsk->bsd', sel, conf)
        return layer_norm(x + combined, out_g, out_b)
    h = _L0_tok_ref(x, L0_tok_W, L0_tok_b)
    h = h + _L0_attn_ref(_layernorm(h, axis=-1), L0_attn_W_Q, L0_attn_W_K, L0_attn_W_V, L0_attn_W_G, L0_attn_W_O, L0_attn_gn_weight, L0_attn_gn_bias)
    h = h + _L0_ffn_ref(_layernorm(h, axis=-1), L0_ffn_Wg, L0_ffn_W1, L0_ffn_b1, L0_ffn_W2, L0_ffn_b2, L0_ffn_ln_g, L0_ffn_ln_b, L0_ffn_out_g, L0_ffn_out_b)
    return h

_drawn_inputs = setup_inputs


def setup_inputs(seed=0):
    import zlib

    import numpy as np

    out = dict(_drawn_inputs(seed))
    spreads = {'L0_attn_gn_weight': (1.0, 0.6),
     'L0_attn_gn_bias': (0.0, 0.8),
     'L0_ffn_b1': (0.0, 0.8),
     'L0_ffn_b2': (0.0, 0.1),
     'L0_ffn_ln_g': (1.0, 0.6),
     'L0_ffn_ln_b': (0.0, 0.562),
     'L0_ffn_out_g': (1.0, 0.2),
     'L0_ffn_out_b': (0.0, 0.1)}
    factors = {'L0_attn_W_G': 8.0, 'L0_ffn_W1': 2.819}
    for name, (base, spread) in spreads.items():
        noise = np.random.default_rng([zlib.crc32(name.encode()), seed]).standard_normal(out[name].shape)
        drawn = base * np.exp(spread * noise) if base else spread * noise
        out[name] = jnp.asarray(drawn.astype(out[name].dtype))
    for name, factor in factors.items():
        out[name] = (out[name] * factor).astype(out[name].dtype)
    return out
```

```python
from contextlib import ExitStack

import numpy as np

import concourse.bass as bass
from concourse import mybir

ALU = mybir.AluOpType
ACT = mybir.ActivationFunctionType
F32 = mybir.dt.float32
BF16 = mybir.dt.bfloat16
U32 = mybir.dt.uint32
AX_X = mybir.AxisListType.X

P = 128
B, S, D = 128, 256, 128
BLOCK, TOPK = 128, 16
ROWS = B * S // BLOCK
HALVES = ROWS // P
T = S // BLOCK * TOPK
TILES = B * T // P
GT = 4
GN = GT * P
G = TILES // GT
HEADS, DH = 8, 16
E, HID = 8, 512
HC = HID // P
EPS = 1e-5
LOWEST = -3.4028234663852886e38
CH = 16
NCH = BLOCK // CH
RING = 4
C_MASK, C_ID = 0, HEADS * P
C_PAR = C_ID + P
C_ROW8 = C_PAR + 2
C_ROW16 = C_ROW8 + 8
C_BASE = C_ROW16 + 16
C_IOTA = C_BASE + 1
C_HALF = C_IOTA + E
C_ALL = C_HALF + 4


def constants():
    c = np.zeros((P, C_ALL), np.float32)
    p = np.arange(P)
    s, t = p[:, None], p[None, :]
    seen = (s // T == t // T) & (t >= s)
    for h in range(HEADS):
        gamma = 1.0 - 2.0 ** (-5.0 - h)
        c[:, C_MASK + h * P:C_MASK + (h + 1) * P] = np.where(seen, gamma ** np.maximum(t - s, 0), 0.0)
    c[:, C_ID:C_ID + P] = np.eye(P)
    c[:, C_PAR] = DH ** -0.5 * (p // DH % 2 == 0)
    c[:, C_PAR + 1] = DH ** -0.5 * (p // DH % 2 == 1)
    c[:, C_ROW8:C_ROW8 + 8] = p[:, None] % 8 == np.arange(8)
    c[:, C_ROW16:C_ROW16 + 16] = p[:, None] // 8 == np.arange(16)
    c[:, C_BASE] = BLOCK * p
    c[:, C_IOTA:C_IOTA + E] = np.arange(E)
    c[:, C_HALF:C_HALF + 4] = -0.5
    return c


ds = bass.ds
SMALL = 14


def program(nc, x, tok_w, tok_b, wq, wk, wv, wg, wo, gn_w, gn_b, ffn_wg, w1, b1, w2, b2,
            ln_g, ln_b, out_g, out_b, consts, out):
    x_chunks = x.rearrange("b (k c t) d -> (b k) c (t d)", c=NCH, t=CH)
    x_tokens = x.rearrange("b s d -> (b s) d")
    out_groups = out.rearrange("b t d -> (b t) d").rearrange("(g j p) d -> g p j d", j=GT, p=P)

    with ExitStack() as ctx:
        def sb(name, shape, dt=F32):
            return ctx.enter_context(nc.sbuf_tensor(name, shape, dt))

        def ps(name, shape):
            return ctx.enter_context(nc.psum_tensor(name, shape, F32))

        def sem(name):
            return ctx.enter_context(nc.semaphore(name))

        cst = sb("cst", [P, C_ALL])
        decay = cst[:, C_MASK:C_MASK + HEADS * P].rearrange("p (j n) -> p j n", j=4)
        ident = cst[:, C_ID:C_ID + P]
        tokw = sb("tokw", [P, D])
        tokb = sb("tokb", [P, 1])
        wq_s, wk_s, wo_s = sb("wq_s", [P, D]), sb("wk_s", [P, D]), sb("wo_s", [P, D])
        wvg = sb("wvg", [P, 2, D])
        vmean = sb("vmean", [P, HEADS])
        gnw, gnb = sb("gnw", [P, D]), sb("gnb", [P, D])
        outg, outb = sb("outg", [P, D]), sb("outb", [P, D])
        lng, lnb = sb("lng", [P, 1]), sb("lnb", [P, 1])
        wgate = sb("wgate", [P, E])
        w1_s = sb("w1_s", [P, E, HID])
        w2_s = sb("w2_s", [P, E, HC, D])
        b1_s = sb("b1_s", [P, E * HC])
        b1_rows = sb("b1_rows", [E * HC, P])
        xring = sb("xring", [P, RING, CH * D])
        product = sb("product", [P, D])
        score = sb("score", [P, BLOCK])
        score2 = sb("score2", [P, BLOCK])
        best = sb("best", [P, TOPK])
        besti = sb("besti", [P, TOPK], U32)
        bestf = sb("bestf", [P, TOPK])
        spread = sb("spread", [P, 8, TOPK])
        index = sb("index", [P, TILES], U32)
        hsel = sb("hsel", [P, TILES, D])
        stats = sb("stats", [P, 2, GT, 6])
        meanvar = sb("meanvar", [P, GT, 2])
        meanvar2 = sb("meanvar2", [P, GT, 2])
        var1 = sb("var1", [P, GT])
        rstd1 = sb("rstd1", [P, GT])
        ln = sb("ln", [P, GT, D])
        lnT = sb("lnT", [P, GN])
        qeo = sb("qeo", [P, 2, GT, 2, P])
        kT = sb("kT", [P, 2, GN])
        vg = sb("vg", [P, 2, GT, 2, D])
        prob = sb("prob", [P, GT, HEADS, P])
        square = sb("square", [P, GN])
        gvar = sb("gvar", [P, GT * HEADS])
        gvar2 = sb("gvar2", [P, GT * HEADS])
        grstd = sb("grstd", [P, GT * HEADS])
        halves = sb("halves", [P, GT * HEADS])
        gate = sb("gate", [P, GT, D])
        normed = sb("normed", [P, GT, D])
        normw = sb("normw", [P, GT, D])
        pre = sb("pre", [P, GT, D])
        th = sb("th", [P, GT, D])
        act_s = sb("act_s", [P, GT, D])
        actT = sb("actT", [P, GN])
        var2, rstd2 = sb("var2", [P, GT]), sb("rstd2", [P, GT])
        var3, rstd3 = sb("var3", [P, GT]), sb("rstd3", [P, GT])
        var4, rstd4 = sb("var4", [P, GT]), sb("rstd4", [P, GT])
        xnTg = sb("xnTg", [P, GN])
        topg, topig = sb("topg", [P, GT, 8]), sb("topig", [P, GT, 8], U32)
        hn2 = sb("hn2", [P, TILES, D])
        xhat = sb("xhat", [P, GT, D])
        xnT = sb("xnT", [P, G, GN])
        logit = sb("logit", [P, GT, E])
        top12 = sb("top12", [P, TILES, 2])
        topif = sb("topif", [P, TILES, 2])
        gap = sb("gap", [P, TILES])
        e2 = sb("e2", [P, TILES])
        esum = sb("esum", [P, TILES])
        conf12 = sb("conf12", [P, TILES, 2])
        pick1, pick2 = sb("pick1", [P, TILES, E]), sb("pick2", [P, TILES, E])
        conf = sb("conf", [P, TILES, E])
        hid = xring[:, :, :].rearrange("p a b -> p (a b)")[:, 0:2 * HC * GN].rearrange("p (a c n) -> p a c n", a=2, c=HC)
        b2hi, b2mid, b2lo = sb("b2hi", [1, E, D], BF16), sb("b2mid", [1, E, D], BF16), sb("b2lo", [1, E, D], BF16)
        b2rest, b2rest2, b2_s = (hn2[0:1, n * E:(n + 1) * E, :] for n in range(3))
        b2_parts = sb("b2_parts", [3, E, D], BF16)
        ones3 = sb("ones3", [3, P], BF16)
        acc, y, yw = ln, act_s, xhat
        yo = sb("yo", [P, 2, GT, D])
        meanvar3 = sb("meanvar3", [P, GT, 2])
        stats3 = sb("stats3", [P, GT, 6])

        bank = [ps(f"bank{i}", [P, 512]) for i in range(4)]
        pscore = ps("pscore", [P, 4, 2, 2 * P])
        ps_t1, ps_a, ps_b, ps_o = bank
        ps_t2, ps_wo, ps_t3, ps_r = (pscore[:, i].rearrange("p a b -> p (a b)") for i in range(4))

        s_cst, s_x0, s_w = sem("s_cst"), sem("s_tokw"), sem("s_weights")
        s_x = [sem(f"s_xchunk{i}") for i in range(RING)]
        s_score = sem("s_score")
        s_top = sem("s_top")
        s_spread = sem("s_spread")
        s_idxps = sem("s_idxps")
        s_index = sem("s_index")
        s_gather = [sem("s_gather0"), sem("s_gather1")]
        s_prep, s_v = sem("s_prep"), sem("s_v")
        s_b1t, s_b1 = sem("s_b1t"), sem("s_b1")
        s_stat1, s_rs1, s_ln = sem("s_stat1"), sem("s_rs1"), sem("s_ln")
        s_pow = sem("s_pow")
        s_t1, s_lnT = sem("s_t1"), sem("s_lnT")
        s_q, s_k, s_vg = sem("s_q"), sem("s_k"), sem("s_vg")
        s_qc, s_kc, s_vgc = sem("s_qc"), sem("s_kc"), sem("s_vgc")
        s_sc, s_prob, s_o = sem("s_sc"), sem("s_prob"), sem("s_o")
        s_sq, s_gvar, s_grs = sem("s_sq"), sem("s_gvar"), sem("s_grs")
        s_gate, s_norm, s_normw, s_pre = sem("s_gate"), sem("s_norm"), sem("s_normw"), sem("s_pre")
        s_th, s_act, s_t2, s_actT = sem("s_th"), sem("s_act"), sem("s_t2"), sem("s_actT")
        s_wo, s_h2, s_stat2, s_rs2, s_xhat = sem("s_wo"), sem("s_h2"), sem("s_stat2"), sem("s_rs2"), sem("s_xhat")
        s_t3, s_xnT, s_r, s_logit = sem("s_t3"), sem("s_xnT"), sem("s_r"), sem("s_logit")
        s_rt = sem("s_router")
        s_e2 = sem("s_e2")
        s_conft, s_confT = sem("s_conft"), sem("s_confT")
        s_up, s_hid, s_down, s_acc = sem("s_up"), sem("s_hid"), sem("s_down"), sem("s_acc")
        s_b2 = sem("s_b2")
        s_y, s_stat3, s_rs3, s_fin = sem("s_y"), sem("s_stat3"), sem("s_rs3"), sem("s_fin")
        s_out = [sem("s_out0"), sem("s_out1")]

        s_half, s_pf, s_ps, s_p3, s_xnTc = sem("s_half"), sem("s_pf"), sem("s_ps"), sem("s_p3"), sem("s_xnTc")
        s_df, s_ds, s_d3, s_hn2 = sem("s_df"), sem("s_ds"), sem("s_d3"), sem("s_hn2")
        s_mx, s_mi, s_tc, s_parts = sem("s_mx"), sem("s_mi"), sem("s_tc"), sem("s_parts")
        s_wbig = sem("s_wbig")
        down = [pscore[:, i].rearrange("p a b -> p (a b)") for i in range(2)]

        block = ctx.enter_context(nc.Block())

        def mix_schedule(eng, first, second):
            first(0, 0)
            first(1, 1)
            second(0, 0)
            with eng.Fori(0, (G - 2) // 2) as i:
                for odd in range(2):
                    g = i * 2 + (1 + odd)
                    first(g + 1, odd)
                    second(g, 1 - odd)
            second(G - 1, (G - 1) % 2)

        @block.sync
        def _(sp):
            sp.dma_start(tokw[:, :], tok_w[0].partition_broadcast(P)).then_inc(s_x0, 16)
            sp.dma_start(tokb[:, :], tok_b.partition_broadcast(P)).then_inc(s_x0, 16)
            for c in range(HALVES * NCH):
                half, k = c // NCH, c % NCH
                if c >= RING:
                    sp.wait_ge(s_score, c - RING + 1)
                sp.dma_start(xring[:, c % RING, :], x_chunks[half * P:(half + 1) * P, k, :]).then_inc(s_x[c % RING], 16)
                if c == 3:
                    sp.dma_start(cst[:, :], consts).then_inc(s_cst, 16)
            sp.wait_ge(s_v, 6)
            for n, part in enumerate((b2hi, b2mid, b2lo)):
                sp.dma_start(b2_parts[n:n + 1, :, :], part[:, :, :]).then_inc(s_parts, 16)
            for e in range(E):
                sp.dma_start(w1_s[:, e, :], w1[e]).then_inc(s_wbig, 16)
                sp.dma_start(w2_s[:, e, :, :], w2[e].rearrange("(c p) d -> p c d", p=P)).then_inc(s_wbig, 16)
            with sp.Fori(0, G // 2) as i:
                for odd in range(2):
                    g = i * 2 + odd
                    sp.wait_ge(s_fin, (g + 1) * (GT + 3))
                    sp.dma_start(out_groups[g], yo[:, odd, :, :]).then_inc(s_out[odd], 16)
            for odd in range(2):
                sp.wait_ge(s_out[odd], 16 * (G // 2) + 1)

        @block.gpsimd
        def _(pool):
            nc.gpsimd.memset(halves[:, :], -0.5).then_inc(s_half, 1)
            pool.wait_ge(s_half, 1)

            def power(dst, base):
                return nc.gpsimd.tensor_tensor(dst, base, halves[:, 0:base.shape[1]], ALU.pow)

            def gather(g):
                if g % (G // HALVES) == 0:
                    pool.wait_ge(s_index, g // (G // HALVES) + 1)
                if g >= 2:
                    pool.wait_ge(s_gather[g % 2], 16 * GT * (g // 2))
                for t in range(g * GT, (g + 1) * GT):
                    nc.gpsimd.indirect_dma_start(
                        out=hsel[:, t, :], out_offset=None, in_=x_tokens,
                        in_offset=bass.IndirectOffsetOnAxis(ap=index[:, t:t + 1], axis=0)).then_inc(s_gather[g % 2], 16)

            def first(g, par):
                pool.wait_ge(s_stat1, g + 1)
                power(rstd1[:, :], var1[:, :]).then_inc(s_rs1, 1)

            def second(g, par):
                pool.wait_ge(s_vgc, g * 2 + 2)
                nc.gpsimd.tensor_tensor(gate[:, :, :], vg[:, par, :, 1, :],
                                        gnb[:, :].unsqueeze(1).to_broadcast([P, GT, D]), ALU.add).then_inc(s_gate, 1)
                pool.wait_ge(s_gvar, g + 1)
                power(grstd[:, :], gvar2[:, :]).then_inc(s_grs, 1)
                pool.wait_ge(s_norm, g + 1)
                nc.gpsimd.tensor_tensor(normw[:, :, :], normed[:, :, :],
                                        gnw[:, :].unsqueeze(1).to_broadcast([P, GT, D]), ALU.mult).then_inc(s_normw, 1)
                pool.wait_ge(s_normw, g + 1)
                pool.wait_ge(s_gate, g + 1)
                nc.gpsimd.tensor_tensor(pre[:, :, :], normw[:, :, :], gate[:, :, :], ALU.add).then_inc(s_pre, 1)
                pool.wait_ge(s_stat2, g * 2 + 2)
                power(rstd2[:, :], var2[:, :]).then_inc(s_rs2, 1)
                power(rstd3[:, :], var3[:, :]).then_inc(s_rs2, 1)
                pool.wait_ge(s_xnT, g + 1)
                nc.gpsimd.tensor_copy(xnT[:, ds(g, 1), :], xnTg[:, :].unsqueeze(1)).then_inc(s_xnTc, 1)

            for g in range(G):
                gather(g)
            mix_schedule(pool, first, second)
            with pool.Fori(0, G) as g:
                pool.wait_ge(s_stat3, g + 1)
                power(rstd4[:, :], var4[:, :]).then_inc(s_rs3, 1)

        @block.scalar
        def _(act):
            small = [(wq_s[:, :], wq), (wk_s[:, :], wk), (wo_s[:, :], wo), (wvg[:, 0, :], wv), (wvg[:, 1, :], wg), (wgate[:, :], ffn_wg),
                     (gnw[:, :], gn_w.partition_broadcast(P)), (gnb[:, :], gn_b.partition_broadcast(P)),
                     (outg[:, :], out_g.partition_broadcast(P)), (outb[:, :], out_b.partition_broadcast(P)),
                     (lng[:, :], ln_g.unsqueeze(1)), (lnb[:, :], ln_b.unsqueeze(1)),
                     (b1_rows[:, :], b1.rearrange("e (c p) -> (e c) p", p=P)), (b2_s[:, :, :], b2.unsqueeze(0))]
            assert len(small) == SMALL
            for dst, src in small:
                act.dma_start(dst, src).then_inc(s_w, 16)

            def first(g, par):
                act.wait_ge(s_t1, g + 1)
                nc.scalar.activation(lnT[:, :], ps_t1[:, :], ACT.Copy).then_inc(s_lnT, 1)
                act.wait_ge(s_q, g + 1)
                for odd in range(2):
                    nc.scalar.activation(qeo[:, par, :, odd, :], ps_a[:, :].rearrange("p (t n) -> p t n", t=GT), ACT.Copy,
                                         scale=cst[:, C_PAR + odd:C_PAR + odd + 1]).then_inc(s_qc, 1)
                act.wait_ge(s_k, g + 1)
                nc.scalar.activation(kT[:, par, :], ps_b[:, :], ACT.Copy).then_inc(s_kc, 1)
                for r, bank_ in enumerate((ps_a, ps_b)):
                    act.wait_ge(s_vg, g * 2 + r + 1)
                    nc.scalar.activation(vg[:, par, 2 * r:2 * r + 2, :, :].rearrange("p a b n -> p (a b n)"),
                                         bank_[:, :], ACT.Copy).then_inc(s_vgc, 1)

            def second(g, par):
                act.wait_ge(s_o, g + 1)
                nc.scalar.activation(square[:, :], ps_o[:, :], ACT.Square).then_inc(s_sq, 1)
                act.wait_ge(s_pre, g + 1)
                nc.scalar.activation(th[:, :, :], pre[:, :, :], ACT.Tanh, scale=0.5).then_inc(s_th, 1)
                act.wait_ge(s_t2, g + 1)
                nc.scalar.activation(actT[:, :], ps_t2, ACT.Copy).then_inc(s_actT, 1)
                act.wait_ge(s_t3, g + 1)
                if not (isinstance(g, int) and g == 0):
                    act.wait_ge(s_xnTc, g + 0)
                nc.scalar.activation(xnTg[:, :], ps_t3, ACT.Identity, scale=lng[:, 0:1], bias=lnb[:, 0:1]).then_inc(s_xnT, 1)

            act.wait_ge(s_cst, 16)
            act.wait_ge(s_w, 16 * SMALL)
            mix_schedule(act, first, second)
            act.wait_ge(s_rt, 1)
            nc.scalar.activation(e2[:, :], gap[:, :], ACT.Exp).then_inc(s_e2, 1)
            act.wait_ge(s_b1, 1)
            with act.Fori(0, G) as g:
                for e in range(E):
                    for c in range(HC):
                        n = e * HC + c
                        act.wait_ge(s_up, g * (E * HC) + n + 1)
                        if n >= 2 * HC and c == 0:
                            act.wait_ge(s_down, g * E + e - 1)
                        nc.scalar.activation(hid[:, e % 2, c, :], bank[n % 4][:, :], ACT.Gelu_apprx_tanh,
                                             bias=b1_s[:, n:n + 1]).then_inc(s_hid, 1)

        @block.vector
        def _(dve):
            dve.wait_ge(s_w, 16 * SMALL)
            wv_heads = wvg[:, 0, :].rearrange("p (h d) -> p h d", h=HEADS)
            nc.vector.tensor_reduce(vmean[:, :], wv_heads, AX_X, ALU.add).then_inc(s_v, 1)
            dve.wait_ge(s_v, 1)
            nc.vector.scalar_tensor_tensor(out=wv_heads, in0=vmean[:, :].unsqueeze(2).to_broadcast([P, HEADS, DH]),
                                           scalar=-1.0 / DH, in1=wv_heads, op0=ALU.mult, op1=ALU.add).then_inc(s_prep, 1)
            nc.vector.tensor_scalar(wo_s[:, :], wo_s[:, :], 0.5, None, ALU.mult).then_inc(s_prep, 1)
            nc.vector.tensor_copy(b2hi[:, :, :], b2_s[:, :, :]).then_inc(s_v, 1)
            dve.wait_ge(s_v, 2)
            nc.vector.tensor_tensor(b2rest[:, :, :], b2_s[:, :, :], b2hi[:, :, :], ALU.subtract).then_inc(s_v, 1)
            dve.wait_ge(s_v, 3)
            nc.vector.tensor_copy(b2mid[:, :, :], b2rest[:, :, :]).then_inc(s_v, 1)
            dve.wait_ge(s_v, 4)
            nc.vector.tensor_tensor(b2rest2[:, :, :], b2rest[:, :, :], b2mid[:, :, :], ALU.subtract).then_inc(s_v, 1)
            dve.wait_ge(s_v, 5)
            nc.vector.tensor_copy(b2lo[:, :, :], b2rest2[:, :, :]).then_inc(s_v, 1)
            nc.vector.memset(ones3[:, :], 1.0).then_inc(s_prep, 1)
            dve.wait_ge(s_b1t, 1)
            nc.vector.tensor_copy(b1_s[:, :], ps_t1[:, 0:E * HC]).then_inc(s_b1, 1)

            dve.wait_ge(s_x0, 32)
            dve.wait_ge(s_cst, 16)
            step = 0
            for half in range(HALVES):
                for k in range(NCH):
                    c = half * NCH + k
                    dve.wait_ge(s_x[c % RING], 16 * (c // RING + 1))
                    for t in range(CH):
                        n = k * CH + t
                        last = nc.vector.tensor_tensor_reduce(
                            out=xring[:, c % RING, t * D:(t + 1) * D], in0=xring[:, c % RING, t * D:(t + 1) * D], in1=tokw[:, :],
                            scale=1.0, scalar=0.0, op0=ALU.mult, op1=ALU.add, accum_out=score[:, n:n + 1])
                    last.then_inc(s_score, 1)

                def chain(instruction):
                    nonlocal step
                    step += 1
                    instruction.then_inc(s_top, 1)
                    dve.wait_ge(s_top, step)

                dve.wait_ge(s_score, (half + 1) * NCH)
                chain(nc.vector.tensor_scalar(score[:, :], score[:, :], tokb[:, 0:1], None, ALU.add))
                chain(nc.vector.max(best[:, 0:8], score[:, :]))
                chain(nc.vector.max_index(besti[:, 0:8], best[:, 0:8], score[:, :]))
                chain(nc.vector.match_replace(score2[:, :], best[:, 0:8], score[:, :], LOWEST))
                chain(nc.vector.max(best[:, 8:16], score2[:, :]))
                chain(nc.vector.max_index(besti[:, 8:16], best[:, 8:16], score2[:, :]))
                chain(nc.vector.tensor_scalar(bestf[:, :], besti[:, :], cst[:, C_BASE:C_BASE + 1], float(half * P * BLOCK),
                                              ALU.add, ALU.add))
                nc.vector.tensor_tensor(spread[:, :, :], bestf[:, :].unsqueeze(1).to_broadcast([P, 8, TOPK]),
                                        cst[:, C_ROW8:C_ROW8 + 8].unsqueeze(2).to_broadcast([P, 8, TOPK]),
                                        ALU.mult).then_inc(s_spread, 1)
                dve.wait_ge(s_idxps, half + 1)
                nc.vector.tensor_copy(index[:, half * 16:half * 16 + 16], ps_t1[:, 0:16]).then_inc(s_index, 1)

            def statistics(stats_, meanvar_, rows):
                for j in range(GT):
                    nc.vector.bn_stats(stats_[:, j, :], rows[j])
                dve.drain()
                for j in range(GT):
                    nc.vector.bn_aggr(meanvar_[:, j, :], stats_[:, j, :])
                dve.drain()

            def first(g, par):
                dve.wait_ge(s_gather[par], (g - par + 2) * (8 * GT))
                rows = [hsel[:, ds(g * GT + j, 1), :].rearrange("p a d -> p (a d)") for j in range(GT)]
                statistics(stats[:, 0], meanvar, rows)
                nc.vector.tensor_scalar(var1[:, :], meanvar[:, :, 1], EPS, None, ALU.add).then_inc(s_stat1, 1)
                dve.wait_ge(s_rs1, g + 1)
                if not (isinstance(g, int) and g == 0):
                    dve.wait_ge(s_t1, g + 0)
                for j in range(GT):
                    nc.vector.tensor_scalar(ln[:, j, :], rows[j], meanvar[:, j, 0:1], rstd1[:, j:j + 1],
                                            ALU.subtract, ALU.mult).then_inc(s_ln, 1)

            def second(g, par):
                for t in range(GT):
                    dve.wait_ge(s_sc, g * GT + t // 2 * 2 + 2)
                    nc.vector.tensor_tensor(prob[:, t, :, :].rearrange("p (j i) n -> p j (i n)", i=2), pscore[:, :, t % 2, :],
                                            decay, ALU.mult).then_inc(s_prob, 1)
                dve.wait_ge(s_sq, g + 1)
                nc.vector.tensor_reduce(gvar[:, :], square[:, :].rearrange("p (a d) -> p a d", d=DH), AX_X, ALU.add)
                dve.drain()
                nc.vector.tensor_scalar(gvar2[:, :], gvar[:, :], 1.0 / DH, EPS, ALU.mult, ALU.add).then_inc(s_gvar, 1)
                dve.wait_ge(s_grs, g + 1)
                nc.vector.tensor_tensor(normed[:, :, :].rearrange("p t (h d) -> p (t h) d", d=DH),
                                        ps_o[:, :].rearrange("p (a d) -> p a d", d=DH),
                                        grstd[:, :].unsqueeze(2).to_broadcast([P, GT * HEADS, DH]), ALU.mult).then_inc(s_norm, 1)
                dve.wait_ge(s_th, g + 1)
                nc.vector.scalar_tensor_tensor(out=act_s[:, :, :], in0=th[:, :, :], scalar=1.0, in1=pre[:, :, :],
                                               op0=ALU.add, op1=ALU.mult).then_inc(s_act, 1)
                dve.wait_ge(s_wo, g + 1)
                tiles = hsel[:, ds(g * GT, GT), :]
                nc.vector.tensor_tensor(tiles, ps_wo.rearrange("p (t d) -> p t d", t=GT), tiles, ALU.add).then_inc(s_h2, 1)
                dve.drain()
                rows = [hsel[:, ds(g * GT + j, 1), :].rearrange("p a d -> p (a d)") for j in range(GT)]
                statistics(stats[:, 1], meanvar2, rows)
                nc.vector.tensor_scalar(var2[:, :], meanvar2[:, :, 1], EPS, None, ALU.add).then_inc(s_stat2, 1)
                nc.vector.tensor_scalar(var3[:, :], meanvar2[:, :, 1], 1.0 + EPS, EPS * EPS,
                                        ALU.mult, ALU.add).then_inc(s_stat2, 1)
                dve.wait_ge(s_rs2, g * 2 + 2)
                for j in range(GT):
                    nc.vector.tensor_scalar(xhat[:, j, :], rows[j], meanvar2[:, j, 0:1], rstd3[:, j:j + 1],
                                            ALU.subtract, ALU.mult).then_inc(s_xhat, 1)
                for j in range(GT):
                    nc.vector.tensor_scalar(hn2[:, ds(g * GT + j, 1), :].rearrange("p a d -> p (a d)"), rows[j],
                                            meanvar2[:, j, 0:1], rstd2[:, j:j + 1],
                                            ALU.subtract, ALU.mult).then_inc(s_hn2, 1)
                dve.wait_ge(s_r, g + 1)
                nc.vector.tensor_copy(logit[:, :, :], ps_r[:, 0:GT * E].rearrange("p (t e) -> p t e", e=E)).then_inc(s_logit, 1)
                dve.drain()
                for j in range(GT):
                    nc.vector.max(topg[:, j, :], logit[:, j, :])
                dve.drain()
                for j in range(GT):
                    nc.vector.max_index(topig[:, j, :], topg[:, j, :], logit[:, j, :]).then_inc(s_mi, 1)
                nc.vector.tensor_copy(top12[:, ds(g * GT, GT), :], topg[:, :, 0:2]).then_inc(s_tc, 1)
                dve.wait_ge(s_mi, (g + 1) * GT)
                nc.vector.tensor_copy(topif[:, ds(g * GT, GT), :], topig[:, :, 0:2]).then_inc(s_tc, 1)

            mix_schedule(dve, first, second)

            dve.wait_ge(s_tc, 2 * G)
            nc.vector.tensor_tensor(gap[:, :], top12[:, :, 1], top12[:, :, 0], ALU.subtract).then_inc(s_rt, 1)
            dve.wait_ge(s_e2, 1)
            nc.vector.tensor_scalar(esum[:, :], e2[:, :], 1.0, None, ALU.add).then_inc(s_rt, 1)
            dve.wait_ge(s_rt, 2)
            nc.vector.reciprocal(conf12[:, :, 0], esum[:, :]).then_inc(s_rt, 1)
            dve.wait_ge(s_rt, 3)
            nc.vector.tensor_tensor(conf12[:, :, 1], conf12[:, :, 0], e2[:, :], ALU.mult).then_inc(s_rt, 1)
            iota = cst[:, C_IOTA:C_IOTA + E].unsqueeze(1).to_broadcast([P, TILES, E])
            for k, pick in enumerate((pick1, pick2)):
                nc.vector.tensor_tensor(pick[:, :, :], iota, topif[:, :, k:k + 1].to_broadcast([P, TILES, E]),
                                        ALU.is_equal).then_inc(s_rt, 1)
            dve.wait_ge(s_rt, 6)
            for k, pick in enumerate((pick1, pick2)):
                nc.vector.tensor_tensor(pick[:, :, :], pick[:, :, :], conf12[:, :, k:k + 1].to_broadcast([P, TILES, E]),
                                        ALU.mult).then_inc(s_rt, 1)
            dve.wait_ge(s_rt, 8)
            nc.vector.tensor_tensor(conf[:, :, :], pick1[:, :, :], pick2[:, :, :], ALU.add).then_inc(s_acc, 1)
            dve.wait_ge(s_acc, 1)
            dve.wait_ge(s_hn2, TILES)

            for odd in range(2):
                dve.sem_inc(s_out[odd], 1)
            with dve.Fori(0, G // 2) as i:
                for odd in range(2):
                    g = i * 2 + odd
                    for e in range(E):
                        dve.wait_ge(s_down, g * E + e + 1)
                        for j in range(GT):
                            scale = conf[:, ds(g * GT + j, 1), e:e + 1].rearrange("p a b -> p (a b)")
                            before = hn2[:, ds(g * GT + j, 1), :].rearrange("p a d -> p (a d)") if e == 0 else acc[:, j, :]
                            if e:
                                dve.wait_ge(s_acc, g * (E * GT) + (e - 1) * GT + j + 2)
                            nc.vector.scalar_tensor_tensor(out=acc[:, j, :], in0=down[e % 2][:, j * D:(j + 1) * D],
                                                           scalar=scale, in1=before,
                                                           op0=ALU.mult, op1=ALU.add).then_inc(s_acc, 1)
                    dve.wait_ge(s_acc, (g + 1) * (E * GT) + 1)
                    statistics(stats3, meanvar3, [acc[:, j, :] for j in range(GT)])
                    nc.vector.tensor_scalar(var4[:, :], meanvar3[:, :, 1], EPS, None, ALU.add).then_inc(s_stat3, 1)
                    dve.wait_ge(s_rs3, g + 1)
                    for j in range(GT):
                        nc.vector.tensor_scalar(y[:, j, :], acc[:, j, :], meanvar3[:, j, 0:1], rstd4[:, j:j + 1],
                                                ALU.subtract, ALU.mult).then_inc(s_fin, 1)
                    dve.wait_ge(s_fin, g * (GT + 3) + GT)
                    nc.vector.tensor_tensor(yw[:, :, :], y[:, :, :], outg[:, :].unsqueeze(1).to_broadcast([P, GT, D]),
                                            ALU.mult).then_inc(s_fin, 1)
                    dve.wait_ge(s_fin, g * (GT + 3) + GT + 1)
                    nc.vector.tensor_tensor(y[:, :, :], yw[:, :, :], outb[:, :].unsqueeze(1).to_broadcast([P, GT, D]),
                                            ALU.add).then_inc(s_fin, 1)
                    dve.wait_ge(s_fin, g * (GT + 3) + GT + 2)
                    dve.wait_ge(s_out[odd], i * 16 + 1)
                    nc.vector.tensor_tensor(yo[:, odd, :, :], y[:, :, :], hsel[:, ds(g * GT, GT), :],
                                            ALU.add).then_inc(s_fin, 1)

        @block.tensor
        def _(pe):
            pe.wait_ge(s_w, 16 * SMALL)
            pe.wait_ge(s_cst, 16)
            pe.transpose(ps_t1[:, 0:E * HC], b1_rows[:, :], ident[0:E * HC, 0:E * HC]).then_inc(s_b1t, 1)
            for half in range(HALVES):
                pe.wait_ge(s_spread, half + 1)
                pe.wait_ge(s_b1, 1)
                if half:
                    pe.wait_ge(s_index, half)
                pe.matmul(ps_t1[:, 0:16], spread[:, :, :].rearrange("p a b -> p (a b)"), cst[:, C_ROW16:C_ROW16 + 16],
                          start=True, stop=True).then_inc(s_idxps, 1)
            pe.wait_ge(s_prep, 3)
            pe.wait_ge(s_index, HALVES)

            def turn(dst, src, done):
                for j in range(GT):
                    last = pe.transpose(dst[:, j * P:(j + 1) * P], src[:, j, :], ident)
                last.then_inc(done, 1)

            def first(g, par):
                pe.wait_ge(s_ln, (g + 1) * GT)
                turn(ps_t1[:, :], ln, s_t1)
                if not (isinstance(g, int) and g == 0):
                    pe.wait_ge(s_vgc, g * 2)
                pe.wait_ge(s_lnT, g + 1)
                pe.matmul(ps_a[:, :], wq_s[:, :], lnT[:, :], start=True, stop=True).then_inc(s_q, 1)
                pe.matmul(ps_b[:, :], wk_s[:, :], lnT[:, :], start=True, stop=True).then_inc(s_k, 1)
                for r, bank_ in enumerate((ps_a, ps_b)):
                    pe.wait_ge(s_kc if r else s_qc, g + 1 if r else g * 2 + 2)
                    for t in range(2):
                        j = 2 * r + t
                        last = pe.matmul(bank_[:, t * 2 * D:(t + 1) * 2 * D], lnT[:, j * P:(j + 1) * P],
                                         wvg[:, :, :].rearrange("p a n -> p (a n)"), start=True, stop=True)
                    last.then_inc(s_vg, 1)

            def second(g, par):
                if not (isinstance(g, int) and g == 0):
                    pe.wait_ge(s_xnT, g + 0)
                    pe.wait_ge(s_logit, g + 0)
                for t in range(GT):
                    if t == 2:
                        pe.wait_ge(s_prob, g * GT + 2)
                    for j in range(4):
                        last = pe.matmul(pscore[:, j, t % 2, :], kT[32 * j:32 * j + 32, par, t * P:(t + 1) * P],
                                         qeo[32 * j:32 * j + 32, par, t, :, :].rearrange("p i n -> p (i n)"),
                                         start=True, stop=True)
                    last.then_inc(s_sc, 1)
                for t in range(GT):
                    pe.wait_ge(s_prob, g * GT + t + 1)
                    for h in range(HEADS):
                        last = pe.matmul(ps_o[:, t * D + h * DH:t * D + (h + 1) * DH], prob[:, t, h, :],
                                         vg[:, par, t, 0, h * DH:(h + 1) * DH], start=True, stop=True)
                last.then_inc(s_o, 1)
                pe.wait_ge(s_act, g + 1)
                turn(ps_t2, act_s, s_t2)
                pe.wait_ge(s_actT, g + 1)
                for j in range(GT):
                    last = pe.matmul(ps_wo[:, j * D:(j + 1) * D], actT[:, j * P:(j + 1) * P], wo_s[:, :], start=True, stop=True)
                last.then_inc(s_wo, 1)
                pe.wait_ge(s_xhat, (g + 1) * GT)
                turn(ps_t3, xhat, s_t3)
                pe.wait_ge(s_xnT, g + 1)
                for j in range(GT):
                    last = pe.matmul(ps_r[:, j * E:(j + 1) * E], xnTg[:, j * P:(j + 1) * P], wgate[:, :], start=True, stop=True)
                last.then_inc(s_r, 1)

            mix_schedule(pe, first, second)
            pe.wait_ge(s_xnTc, G)
            pe.wait_ge(s_logit, G)
            pe.wait_ge(s_wbig, 16 * 2 * E)
            pe.wait_ge(s_parts, 48)
            with pe.Fori(0, G) as g:
                def up(e):
                    for c in range(HC):
                        n = e * HC + c
                        if n >= 4:
                            pe.wait_ge(s_hid, g * (E * HC) + n - 3)
                        pe.matmul(bank[n % 4][:, :], w1_s[:, e, c * P:(c + 1) * P],
                                  xnT[:, ds(g, 1), :].rearrange("p a n -> p (a n)"), start=True, stop=True).then_inc(s_up, 1)

                def lower(e):
                    pe.wait_ge(s_hid, g * (E * HC) + (e + 1) * HC)
                    pe.wait_ge(s_acc, g * (E * GT) + max(e - 1, 0) * GT + 1)
                    for j in range(GT):
                        dst = down[e % 2][:, j * D:(j + 1) * D]
                        pe.matmul(dst, ones3[:, :], b2_parts[:, e, :], start=True, stop=False)
                        for c in range(HC):
                            last = pe.matmul(dst, hid[:, e % 2, c, j * P:(j + 1) * P], w2_s[:, e, c, :],
                                             start=False, stop=(c == HC - 1))
                    last.then_inc(s_down, 1)

                up(0)
                for e in range(E):
                    if e + 1 < E:
                        up(e + 1)
                    lower(e)


_INS = ["x", "L0_tok_W", "L0_tok_b", "L0_attn_W_Q", "L0_attn_W_K", "L0_attn_W_V", "L0_attn_W_G", "L0_attn_W_O",
        "L0_attn_gn_weight", "L0_attn_gn_bias", "L0_ffn_Wg", "L0_ffn_W1", "L0_ffn_b1", "L0_ffn_W2", "L0_ffn_b2",
        "L0_ffn_ln_g", "L0_ffn_ln_b", "L0_ffn_out_g", "L0_ffn_out_b"]


def kernel(**inputs):
    import concourse.bacc as bacc
    from concourse.bass_utils import run_bass_kernel_spmd

    nc = bacc.Bacc("TRN2", target_bir_lowering=False, num_devices=1)
    arrays = {name: np.ascontiguousarray(inputs[name]) for name in _INS}
    arrays["consts"] = constants()
    args = [nc.dram_tensor(name, a.shape, mybir.dt.from_np(a.dtype), kind="ExternalInput").ap()
            for name, a in arrays.items()]
    out = nc.dram_tensor("out", (B, T, D), F32, kind="ExternalOutput").ap()
    program(nc, *args, out)
    return run_bass_kernel_spmd(nc, [arrays], core_ids=[0]).results[0]["out"]
```

```python
from contextlib import ExitStack

import numpy as np

import concourse.bass as bass
from concourse import mybir

ALU = mybir.AluOpType
ACT = mybir.ActivationFunctionType
F32 = mybir.dt.float32
BF16 = mybir.dt.bfloat16
U32 = mybir.dt.uint32
I32 = mybir.dt.int32
AX_X = mybir.AxisListType.X

P = 128
B, S, D = 128, 256, 128
BLOCK, TOPK = 128, 16
ROWS = B * S // BLOCK
HALVES = ROWS // P
T = S // BLOCK * TOPK
TILES = B * T // P
GT = 4
GN = GT * P
G = TILES // GT
HEADS, DH = 8, 16
E, HID = 8, 512
HC = HID // P
EPS = 1e-5
REGION = TILES * P + P
PAIRS = 2 * TILES * P
SLOTS = 2 * TILES + E - 1
XW = D + 2
LOWEST = -3.4028234663852886e38
CH = 16
NCH = BLOCK // CH
RING = 5
C_MASK, C_ID = 0, HEADS * P
C_PAR = C_ID + P
C_ROW8 = C_PAR + 2
C_ROW16 = C_ROW8 + 8
C_BASE = C_ROW16 + 16
C_IOTA = C_BASE + 1
C_REGION = C_IOTA + E
C_PAD = C_REGION + E
C_TOKEN = C_PAD + E
C_TRI8 = C_TOKEN + GT
C_TILE = C_TRI8 + E * E
C_SLOT = C_TILE + TILES
C_EARLIER = C_SLOT + 1
C_ALL = C_EARLIER + P


def constants():
    c = np.zeros((P, C_ALL), np.float32)
    p = np.arange(P)
    s, t = p[:, None], p[None, :]
    seen = (s // T == t // T) & (t >= s)
    for h in range(HEADS):
        gamma = 1.0 - 2.0 ** (-5.0 - h)
        c[:, C_MASK + h * P:C_MASK + (h + 1) * P] = np.where(seen, gamma ** np.maximum(t - s, 0), 0.0)
    c[:, C_ID:C_ID + P] = np.eye(P)
    c[:, C_PAR] = DH ** -0.5 * (p // DH % 2 == 0)
    c[:, C_PAR + 1] = DH ** -0.5 * (p // DH % 2 == 1)
    c[:, C_ROW8:C_ROW8 + 8] = p[:, None] % 8 == np.arange(8)
    c[:, C_ROW16:C_ROW16 + 16] = p[:, None] // 8 == np.arange(16)
    c[:, C_BASE] = BLOCK * p
    c[:, C_IOTA:C_IOTA + E] = np.arange(E)
    c[:, C_REGION:C_REGION + E] = REGION * np.arange(E)
    c[:, C_PAD:C_PAD + E] = REGION * np.arange(E) + s
    c[:, C_TOKEN:C_TOKEN + GT] = 2 * (P * np.arange(GT) + s)
    c[:, C_TRI8:C_TRI8 + E * E] = (np.arange(E)[None, :] <= np.arange(E)[:, None]).reshape(-1)
    c[:, C_TILE:C_TILE + TILES] = P * np.arange(TILES)
    c[:, C_SLOT] = p
    c[:, C_EARLIER:C_EARLIER + P] = s < t
    return c


ds = bass.ds
SMALL = 14


def program(nc, x, tok_w, tok_b, wq, wk, wv, wg, wo, gn_w, gn_b, ffn_wg, w1, b1, w2, b2,
            ln_g, ln_b, out_g, out_b, consts, out, routed, pairs):
    x_chunks = x.rearrange("b (k c t) d -> (b k) c (t d)", c=NCH, t=CH)
    x_tokens = x.rearrange("b s d -> (b s) d")
    out_groups = out.rearrange("b t d -> (b t) d").rearrange("(g j p) d -> g p j d", j=GT, p=P)

    pair_groups = pairs.rearrange("(g j p k) d -> g p j k d", j=GT, p=P, k=2)

    with ExitStack() as ctx:
        def sb(name, shape, dt=F32):
            return ctx.enter_context(nc.sbuf_tensor(name, shape, dt))

        def ps(name, shape):
            return ctx.enter_context(nc.psum_tensor(name, shape, F32))

        def sem(name):
            return ctx.enter_context(nc.semaphore(name))

        cst = sb("cst", [P, C_ALL])
        decay = cst[:, C_MASK:C_MASK + HEADS * P].rearrange("p (j n) -> p j n", j=4)
        ident = cst[:, C_ID:C_ID + P]
        tokw = sb("tokw", [P, D])
        tokb = sb("tokb", [P, 1])
        wq_s, wk_s, wo_s = sb("wq_s", [P, D]), sb("wk_s", [P, D]), sb("wo_s", [P, D])
        wvg = sb("wvg", [P, 2, D])
        vmean = sb("vmean", [P, HEADS])
        gnw, gnb = sb("gnw", [P, D]), sb("gnb", [P, D])
        outg, outb = sb("outg", [P, D]), sb("outb", [P, D])
        lng, lnb = sb("lng", [P, 1]), sb("lnb", [P, 1])
        wgate = sb("wgate", [P, E])
        w1_s = sb("w1_s", [P, E, HID + HC])
        w2_s = sb("w2_s", [P, E, HC, D])
        b1_rows = sb("b1_rows", [E * HC, P])
        xring = sb("xring", [P, RING, CH * D])
        score = sb("score", [P, HALVES, BLOCK])
        score2 = sb("score2", [P, BLOCK])
        best = sb("best", [P, TOPK])
        besti = sb("besti", [P, TOPK], U32)
        bestf = sb("bestf", [P, TOPK])
        spread = sb("spread", [P, 8, TOPK])
        index = sb("index", [P, TILES], U32)
        hsel = sb("hsel", [P, TILES, D])
        stats = sb("stats", [P, 2, GT, 6])
        meanvar = sb("meanvar", [P, GT, 2])
        meanvar2 = sb("meanvar2", [P, GT, 2])
        var1 = sb("var1", [P, GT])
        rstd1, nm1 = sb("rstd1", [P, GT]), sb("nm1", [P, GT])
        nm2, nm3 = sb("nm2", [P, GT]), sb("nm3", [P, GT])
        ln = sb("ln", [P, GT, D])
        lnT = sb("lnT", [P, GN])
        qeo = sb("qeo", [P, GT, 2, P])
        kT = sb("kT", [P, GN])
        vpad = sb("vpad", [P, GT, 2, D])
        gts = sb("gts", [P, GT, D])
        retT = sb("retT", [P, GT, P])
        prob = sb("prob", [P, GT, HEADS, P])
        square = sb("square", [P, GN])
        gvar = sb("gvar", [P, GT * HEADS])
        gvar2 = sb("gvar2", [P, GT * HEADS])
        grstd = sb("grstd", [P, GT * HEADS])
        halves = sb("halves", [P, GT * HEADS])
        gate = sb("gate", [P, GT, D])
        normed = sb("normed", [P, GT, D])
        normw = sb("normw", [P, GT, D])
        pre = sb("pre", [P, GT, D])
        th = sb("th", [P, GT, D])
        act_s = sb("act_s", [P, GT, D])
        actT = sb("actT", [P, GN])
        var2, rstd2 = sb("var2", [P, GT]), sb("rstd2", [P, GT])
        var3, rstd3 = sb("var3", [P, GT]), sb("rstd3", [P, GT])
        var4, rstd4 = sb("var4", [P, 2, GT]), sb("rstd4", [P, 2, GT])
        xnTg = sb("xnTg", [P, GN])
        topg, topig = sb("topg", [P, GT, 8]), sb("topig", [P, GT, 8], U32)
        hn2 = sb("hn2", [P, TILES, D])
        xhat = sb("xhat", [P, GT, D])
        logit = sb("logit", [P, GT, E])
        top12 = sb("top12", [P, TILES, 2])
        gap = sb("gap", [P, TILES])
        e2 = sb("e2", [P, TILES])
        esum = sb("esum", [P, TILES])
        conf12 = sb("conf12", [P, TILES, 2])
        topf = sb("topf", [P, 2, GT])
        pick = sb("pick", [P, 2, GT, E])
        chosen = sb("chosen", [P, GT, E], BF16)
        chosen_sum = sb("chosen_sum", [P, E])
        before = sb("before", [P, E], BF16)
        earlier, ones = sb("earlier", [P, P], BF16), sb("ones", [P, P], BF16)
        rank = sb("rank", [P, GT, E])
        rank_pick = sb("rank_pick", [P, 2, GT, E])
        posf = sb("posf", [P, 2, GT])
        pos = sb("pos", [P, 2 * GT], U32)
        xrow = sb("xrow", [P, 2, GT, XW])
        zrow = sb("zrow", [P, XW])
        count = sb("count", [P, E])
        padpos = sb("padpos", [P, E], U32)
        reached, ntiles = sb("reached", [P, E, TILES]), sb("ntiles", [P, E])
        tri, ends = sb("tri", [P, E, E]), sb("ends", [P, E])
        passed, jump, jumps = sb("passed", [P, E]), sb("jump", [P, E]), sb("jumps", [P, E])
        slot_row, slot_e, slot_in = sb("slot_row", [P, 1]), sb("slot_e", [P, 1]), sb("slot_in", [P, 1])
        slot_cols = sb("slot_cols", [P, 2])
        table = sb("table", [1, 2 * P], I32)
        xin = sb("xin", [P, 4, XW])
        ids, dest = sb("ids", [P, 4, 2], U32), sb("dest", [P, 4], U32)
        xT = sb("xT", [P, 2, P])
        w1_now = sb("w1_now", [P, 2, HID + HC])
        hid = sb("hid", [P, 2, HC, P])
        yslot = sb("yslot", [P, 4, D])
        ypair = xring[:, :, :].rearrange("p a b -> p (a b)")[:, 0:G * GT * 2 * D].rearrange(
            "p (g t k d) -> p g t k d", g=G, t=GT, k=2)
        b2hi, b2mid, b2lo = sb("b2hi", [1, E, D], BF16), sb("b2mid", [1, E, D], BF16), sb("b2lo", [1, E, D], BF16)
        b2rest, b2rest2, b2_s = (hn2[0:1, n * E:(n + 1) * E, :] for n in range(3))
        b2_parts = sb("b2_parts", [3, E, D], BF16)
        ones3 = sb("ones3", [3, P], BF16)
        acc1 = [th, gts]
        acc, y, yw = [ln, normed], [act_s, pre], [normw, gate]
        nm4 = sb("nm4", [P, 2, GT])
        yo = prob[:, 0].rearrange("p (a t) d -> p a t d", a=2)
        meanvar3 = [meanvar, meanvar2]
        stats3 = sb("stats3", [P, GT, 6])

        bank = [ps(f"bank{i}", [P, 512]) for i in range(4)]
        pscore = ps("pscore", [P, 4, 2, 2 * P])
        ps_ret, ps_a, ps_b, ps_c = bank

        s_cst, s_x0, s_w = sem("s_cst"), sem("s_tokw"), sem("s_weights")
        s_x = [sem(f"s_xchunk{i}") for i in range(RING)]
        s_score = sem("s_score")
        s_top = sem("s_top")
        s_spread = sem("s_spread")
        s_idxps = sem("s_idxps")
        s_index = sem("s_index")
        s_gather = [sem(f"s_gather{g}") for g in range(G)]
        s_prep = sem("s_prep")
        s_b1t, s_b1 = sem("s_b1t"), sem("s_b1")
        s_scoreA, s_prod, s_zero = sem("s_scoreA"), sem("s_prod"), sem("s_zero")
        s_stat1, s_rs1, s_nm1, s_ln = sem("s_stat1"), sem("s_rs1"), sem("s_nm1"), sem("s_ln")
        s_t1, s_lnT, s_q, s_k, s_v, s_g = (sem(n) for n in ("s_t1", "s_lnT", "s_q", "s_k", "s_v", "s_g"))
        s_qc, s_kc, s_vc, s_gc = (sem(n) for n in ("s_qc", "s_kc", "s_vc", "s_gc"))
        s_sc, s_prob, s_ret, s_retc, s_tret = (sem(n) for n in ("s_sc", "s_prob", "s_ret", "s_retc", "s_tret"))
        s_sq, s_gvar, s_grs = sem("s_sq"), sem("s_gvar"), sem("s_grs")
        s_gate, s_norm, s_normw, s_pre = sem("s_gate"), sem("s_norm"), sem("s_normw"), sem("s_pre")
        s_th, s_act, s_tz, s_zT, s_wo = (sem(n) for n in ("s_th", "s_act", "s_tz", "s_zT", "s_wo"))
        s_stat2, s_rs2, s_nm2, s_xhat, s_hn2 = (sem(n) for n in ("s_stat2", "s_rs2", "s_nm2", "s_xhat", "s_hn2"))
        s_t3, s_xnT, s_r, s_logit, s_tc = (sem(n) for n in ("s_t3", "s_xnT", "s_r", "s_logit", "s_tc"))
        s_rt = sem("s_router")
        s_e2 = sem("s_e2")
        s_pick, s_rank, s_rankc, s_pos, s_row = (sem(n) for n in ("s_pick", "s_rank", "s_rankc", "s_pos", "s_row"))
        s_scat, s_zrow, s_pad, s_ztile = sem("s_scattered"), sem("s_zero_rows"), sem("s_padded"), sem("s_zero_tile")
        s_cnt, s_slot, s_tab, s_tabT = sem("s_counts"), sem("s_slot"), sem("s_table"), sem("s_tableT")
        s_xin = [sem(f"s_xin{u}") for u in range(4)]
        s_pairs = [sem(f"s_pairs{u}") for u in range(4)]
        s_ids, s_dest = sem("s_ids"), sem("s_dest")
        s_xt, s_xTc, s_w1, s_up, s_hid, s_down, s_y = (sem(n) for n in ("s_xt", "s_xTc", "s_w1", "s_up", "s_hid", "s_down", "s_y"))
        s_load = [sem("s_load0"), sem("s_load1")]
        s_acc1, s_acc, s_stat3, s_rs4, s_nm4, s_norm4, s_mul4, s_fin = (sem(n) for n in (
            "s_acc1", "s_acc", "s_stat3", "s_rs4", "s_nm4", "s_norm4", "s_mul4", "s_fin"))
        s_hb = sem("s_hb")
        s_out = [sem("s_out0"), sem("s_out1")]

        s_half, s_w0, s_parts = sem("s_half"), sem("s_w0"), sem("s_parts")
        s_wbig = sem("s_wbig")
        down = [pscore[:, i].rearrange("p a b -> p (a b)") for i in range(2)]

        block = ctx.enter_context(nc.Block())

        def chunks_of(half, owner):
            return [half * NCH + k for k in range(NCH) if (k % 3 == 2 or k == 0) == bool(owner)]

        def here(p):
            return not isinstance(p, int) or 0 <= p < G

        def mix_schedule(eng, step):
            for i in range(-2, 3):
                step(i)
            with eng.Fori(3, G - 2) as i:
                step(i)
            for i in range(G - 2, G + 3):
                step(i)

        def repeat(eng, step, count, unroll):
            last = (count - 1) // unroll
            for u in range(unroll):
                step(0, u)
            with eng.Fori(1, last) as i:
                for u in range(unroll):
                    step(i, u)
            for u in range(count - last * unroll):
                step(last, u)

        def exists(n, count):
            return not isinstance(n, int) or 0 <= n < count

        def ahead(i, u, by, unroll):
            i, u = i + (u + by) // unroll, (u + by) % unroll
            return i * unroll + u, i, u

        def used_up(eng, c):
            for owner, s_used in enumerate((s_score, s_scoreA)):
                mine = [n for h in range(HALVES) for n in chunks_of(h, owner)]
                if c in mine:
                    eng.wait_ge(s_used, mine.index(c) + 1)

        def scored(eng, half):
            for owner, s_used in enumerate((s_score, s_scoreA)):
                eng.wait_ge(s_used, sum(len(chunks_of(h, owner)) for h in range(half + 1)))

        @block.sync
        def _(sp):
            sp.dma_start(tokw[:, :], tok_w[0].partition_broadcast(P)).then_inc(s_x0, 16)
            sp.dma_start(tokb[:, :], tok_b.partition_broadcast(P)).then_inc(s_x0, 16)
            for c in range(HALVES * NCH):
                half, k = c // NCH, c % NCH
                if c >= RING:
                    used_up(sp, c - RING)
                sp.dma_start(xring[:, c % RING, :], x_chunks[half * P:(half + 1) * P, k, :]).then_inc(s_x[c % RING], 16)
                if c == 3:
                    sp.dma_start(cst[:, :], consts).then_inc(s_cst, 16)
            sp.wait_ge(s_w0, 6)
            for n, part in enumerate((b2hi, b2mid, b2lo)):
                sp.dma_start(b2_parts[n:n + 1, :, :], part[:, :, :]).then_inc(s_parts, 16)
            for e in range(E):
                sp.dma_start(w1_s[:, e, 0:HID], w1[e]).then_inc(s_wbig, 16)
                sp.dma_start(w2_s[:, e, :, :], w2[e].rearrange("(c p) d -> p c d", p=P)).then_inc(s_wbig, 16)
            sp.wait_ge(s_zrow, 2)
            sp.dma_start(routed[E * REGION:E * REGION + P, :], zrow[:, :]).then_inc(s_ztile, 16)
            sp.wait_ge(s_tabT, 1)
            sp.wait_ge(s_scat, 16 * 2 * TILES)
            sp.wait_ge(s_pad, 16 * E)
            sp.wait_ge(s_ztile, 16)

            def load_slot(i, u):
                s = i * 4 + u
                row = sp.value_load(table[0:1, ds(s, 1)], min_val=0, max_val=E * REGION)
                if exists(s - 4, SLOTS):
                    sp.wait_ge(s_xt, s - 3)
                    sp.wait_ge(s_ids, s - 3)
                sp.dma_start(xin[:, u, :], routed[ds(row, P), :]).then_inc(s_xin[u], 16)

            repeat(sp, load_slot, SLOTS, 4)
            for u in range(4):
                sp.wait_ge(s_pairs[u], 16 * len(range(u, SLOTS, 4)))
            for g in range(G):
                if g >= 2:
                    sp.wait_ge(s_load[g % 2], 16 * (g // 2))
                sp.dma_start(ypair[:, g, :, :, :], pair_groups[g]).then_inc(s_load[g % 2], 16)

            def store(i, odd):
                g = i * 2 + odd
                sp.wait_ge(s_fin, g + 1)
                sp.dma_start(out_groups[g], yo[:, odd, :, :]).then_inc(s_out[odd], 16)

            repeat(sp, store, G, 2)
            for odd in range(2):
                sp.wait_ge(s_out[odd], 16 * (G // 2))

        @block.gpsimd
        def _(pool):
            nc.gpsimd.memset(vpad[:, :, :, :], 0.0).then_inc(s_zero, 1)
            nc.gpsimd.memset(halves[:, :], -0.5).then_inc(s_half, 1)
            pool.wait_ge(s_half, 1)

            def power(dst, base):
                return nc.gpsimd.tensor_tensor(dst, base, halves[:, 0:base.shape[1]], ALU.pow)

            def products(half):
                for c in chunks_of(half, 1):
                    pool.wait_ge(s_x[c % RING], 16 * (c // RING + 1))
                    rows = xring[:, c % RING, :].rearrange("p (t d) -> p t d", d=D)
                    nc.gpsimd.tensor_tensor(rows, rows, tokw[:, :].unsqueeze(1).to_broadcast([P, CH, D]),
                                            ALU.mult).then_inc(s_prod, 1)

            def gather(g):
                for t in range(g * GT, (g + 1) * GT):
                    nc.gpsimd.indirect_dma_start(
                        out=hsel[:, t, :], out_offset=None, in_=x_tokens,
                        in_offset=bass.IndirectOffsetOnAxis(ap=index[:, t:t + 1], axis=0)).then_inc(s_gather[g], 16)

            def scatter(choice):
                for t in range(GT):
                    n = choice * GT + t
                    nc.gpsimd.indirect_dma_start(
                        out=routed, out_offset=bass.IndirectOffsetOnAxis(ap=pos[:, n:n + 1], axis=0),
                        in_=xrow[:, choice, t, :], in_offset=None).then_inc(s_scat, 16)

            def step(i):
                if here(i - 1):
                    if here(i - 2):
                        pool.wait_ge(s_pre, i - 1)
                    pool.wait_ge(s_gc, i)
                    nc.gpsimd.tensor_tensor(gate[:, :, :], gts[:, :, :],
                                            gnb[:, :].unsqueeze(1).to_broadcast([P, GT, D]), ALU.add).then_inc(s_gate, 1)
                if isinstance(i, int) and i == 2:
                    pool.wait_ge(s_index, 2)
                    for g in range(G // 2, G):
                        gather(g)
                if here(i - 2):
                    pool.wait_ge(s_stat2, (i - 2) * 2 + 2)
                    power(rstd2[:, :], var2[:, :]).then_inc(s_rs2, 1)
                    power(rstd3[:, :], var3[:, :]).then_inc(s_rs2, 1)
                if here(i - 1):
                    pool.wait_ge(s_gvar, i)
                    power(grstd[:, :], gvar2[:, :]).then_inc(s_grs, 1)
                    pool.wait_ge(s_norm, i)
                    nc.gpsimd.tensor_tensor(normw[:, :, :], normed[:, :, :],
                                            gnw[:, :].unsqueeze(1).to_broadcast([P, GT, D]), ALU.mult).then_inc(s_normw, 1)
                    pool.wait_ge(s_normw, i)
                    pool.wait_ge(s_gate, i)
                    if here(i - 3):
                        pool.wait_ge(s_pos, i - 2)
                    nc.gpsimd.tensor_tensor(pre[:, :, :], normw[:, :, :], gate[:, :, :], ALU.add).then_inc(s_pre, 1)
                if here(i + 2):
                    pool.wait_ge(s_stat1, i + 3)
                    power(rstd1[:, :], var1[:, :]).then_inc(s_rs1, 1)
                if here(i - 3):
                    if not here(i - 1):
                        pool.wait_ge(s_pos, i - 2)
                    scatter(0)
                    scatter(1)

            pool.wait_ge(s_x0, 32)
            products(0)
            pool.wait_ge(s_index, 1)
            for g in range(G // 2):
                gather(g)
            products(1)
            mix_schedule(pool, step)
            pool.wait_ge(s_zrow, 2)
            pool.wait_ge(s_cnt, 2)
            for e in range(E):
                nc.gpsimd.indirect_dma_start(
                    out=routed, out_offset=bass.IndirectOffsetOnAxis(ap=padpos[:, e:e + 1], axis=0),
                    in_=zrow[:, :], in_offset=None).then_inc(s_pad, 16)

            def place(n, u):
                pool.wait_ge(s_ids, n + 1)
                nc.gpsimd.tensor_tensor(dest[:, u:u + 1], ids[:, u, 0:1], ids[:, u, 1:2], ALU.add).then_inc(s_dest, 1)

            def scatter_slot(i, u):
                s = i * 4 + u
                pool.wait_ge(s_dest, s + 1)
                pool.wait_ge(s_y, s + 1)
                n, _, v = ahead(i, u, 1, 4)
                if exists(n, SLOTS):
                    place(n, v)
                nc.gpsimd.indirect_dma_start(
                    out=pairs, out_offset=bass.IndirectOffsetOnAxis(ap=dest[:, u:u + 1], axis=0),
                    in_=yslot[:, u, :], in_offset=None,
                    bounds_check=PAIRS - 1, oob_is_err=False).then_inc(s_pairs[u], 16)

            place(0, 0)
            repeat(pool, scatter_slot, SLOTS, 4)

            def finish(i, odd):
                g = i * 2 + odd
                pool.wait_ge(s_stat3, g + 1)
                power(rstd4[:, odd, :], var4[:, odd, :]).then_inc(s_rs4, 1)
                pool.wait_ge(s_norm4, g + 1)
                if exists(g - 2, G):
                    pool.wait_ge(s_fin, g - 1)
                nc.gpsimd.tensor_tensor(yw[odd][:, :, :], y[odd][:, :, :], outg[:, :].unsqueeze(1).to_broadcast([P, GT, D]),
                                        ALU.mult).then_inc(s_mul4, 1)

            repeat(pool, finish, G, 2)

        @block.scalar
        def _(act):
            small = [(wq_s[:, :], wq), (wk_s[:, :], wk), (wo_s[:, :], wo), (wvg[:, 0, :], wv), (wvg[:, 1, :], wg), (wgate[:, :], ffn_wg),
                     (gnw[:, :], gn_w.partition_broadcast(P)), (gnb[:, :], gn_b.partition_broadcast(P)),
                     (outg[:, :], out_g.partition_broadcast(P)), (outb[:, :], out_b.partition_broadcast(P)),
                     (lng[:, :], ln_g.unsqueeze(1)), (lnb[:, :], ln_b.unsqueeze(1)),
                     (b1_rows[:, :], b1.rearrange("e (c p) -> (e c) p", p=P)), (b2_s[:, :, :], b2.unsqueeze(0))]
            assert len(small) == SMALL
            for dst, src in small:
                act.dma_start(dst, src).then_inc(s_w, 16)

            def hsel_g(g, j):
                return hsel[:, ds(g * GT + j, 1), :].rearrange("p a d -> p (a d)")

            def sums(half):
                for c in chunks_of(half, 1):
                    act.wait_ge(s_prod, [n for h in range(HALVES) for n in chunks_of(h, 1)].index(c) + 1)
                    for t in range(CH):
                        row = xring[:, c % RING, t * D:(t + 1) * D]
                        n = c % NCH * CH + t
                        last = nc.scalar.activation(row, row, ACT.Copy, accum_out=score[:, half, n:n + 1])
                    last.then_inc(s_scoreA, 1)

            def step(i):
                if here(i - 2):
                    act.wait_ge(s_tz, i - 1)
                    nc.scalar.activation(actT[:, :], ps_b[:, :], ACT.Copy).then_inc(s_zT, 1)
                if here(i - 1):
                    act.wait_ge(s_ret, i)
                    nc.scalar.activation(retT[:, :, :].rearrange("p a b -> p (a b)"), ps_ret[:, :], ACT.Copy).then_inc(s_retc, 1)
                if here(i):
                    act.wait_ge(s_v, i + 1)
                    heads = ps_a[:, :].rearrange("p (t h e d) -> p t h e d", t=GT, e=2, d=DH)
                    if isinstance(i, int) and i == 0:
                        act.wait_ge(s_zero, 1)
                    for odd in range(2):
                        nc.scalar.activation(vpad[:, :, odd, :].rearrange("p t (h e d) -> p t h e d", e=2, d=DH)[:, :, :, odd, :],
                                             heads[:, :, :, odd, :], ACT.Copy).then_inc(s_vc, 1)
                    act.wait_ge(s_g, i + 1)
                    if here(i - 1):
                        act.wait_ge(s_gate, i)
                    nc.scalar.activation(gts[:, :, :].rearrange("p a b -> p (a b)"), ps_b[:, :], ACT.Copy).then_inc(s_gc, 1)
                if here(i - 1):
                    act.wait_ge(s_tret, i)
                    if here(i - 2):
                        act.wait_ge(s_gvar, i - 1)
                    nc.scalar.activation(square[:, :], ps_a[:, :], ACT.Square).then_inc(s_sq, 1)
                if here(i + 1):
                    act.wait_ge(s_t1, i + 2)
                    nc.scalar.activation(lnT[:, :], ps_b[:, :], ACT.Copy).then_inc(s_lnT, 1)
                if here(i - 2):
                    act.wait_ge(s_nm2, (i - 2) * 2 + 2)
                    if here(i - 3):
                        act.wait_ge(s_t3, i - 2)
                        act.wait_ge(s_row, i - 2)
                    for j in range(GT):
                        last = nc.scalar.activation(xhat[:, j, :], hsel_g(i - 2, j), ACT.Identity,
                                                    scale=rstd3[:, j:j + 1], bias=nm3[:, j:j + 1])
                    last.then_inc(s_xhat, 1)
                    for j in range(GT):
                        nc.scalar.activation(hn2[:, ds((i - 2) * GT + j, 1), :].rearrange("p a d -> p (a d)"), hsel_g(i - 2, j),
                                             ACT.Identity, scale=rstd2[:, j:j + 1], bias=nm2[:, j:j + 1]).then_inc(s_hn2, 1)
                    act.wait_ge(s_t3, i - 1)
                    nc.scalar.activation(xnTg[:, :], ps_c[:, :], ACT.Identity,
                                         scale=lng[:, 0:1], bias=lnb[:, 0:1]).then_inc(s_xnT, 1)
                if here(i + 1):
                    act.wait_ge(s_k, i + 2)
                    nc.scalar.activation(kT[:, :], ps_b[:, :], ACT.Copy).then_inc(s_kc, 1)
                    act.wait_ge(s_q, i + 2)
                    for odd in range(2):
                        nc.scalar.activation(qeo[:, :, odd, :], ps_c[:, :].rearrange("p (t n) -> p t n", t=GT), ACT.Copy,
                                             scale=cst[:, C_PAR + odd:C_PAR + odd + 1]).then_inc(s_qc, 1)
                if here(i - 1):
                    act.wait_ge(s_pre, i)
                    nc.scalar.activation(th[:, :, :], pre[:, :, :], ACT.Tanh, scale=0.5).then_inc(s_th, 1)
                if here(i + 2):
                    act.wait_ge(s_nm1, i + 3)
                    if here(i + 1):
                        act.wait_ge(s_t1, i + 2)
                    for j in range(GT):
                        last = nc.scalar.activation(ln[:, j, :], hsel_g(i + 2, j), ACT.Identity,
                                                    scale=rstd1[:, j:j + 1], bias=nm1[:, j:j + 1])
                    last.then_inc(s_ln, 1)

            act.wait_ge(s_cst, 16)
            act.wait_ge(s_w, 16 * SMALL)
            sums(0)
            sums(1)
            mix_schedule(act, step)
            act.wait_ge(s_rt, 1)
            nc.scalar.activation(e2[:, :], gap[:, :], ACT.Exp).then_inc(s_e2, 1)

            def xT_out(n, u):
                act.wait_ge(s_xt, n + 1)
                if exists(n - 2, SLOTS):
                    act.wait_ge(s_up, n - 1)
                nc.scalar.activation(xT[:, u % 2, :], bank[u % 2][:, 0:P], ACT.Identity,
                                     scale=lng[:, 0:1], bias=lnb[:, 0:1]).then_inc(s_xTc, 1)

            def hidden(n, u):
                act.wait_ge(s_up, n + 1)
                if exists(n - 2, SLOTS):
                    act.wait_ge(s_down, n - 1)
                for c in range(HC):
                    nc.scalar.activation(hid[:, u % 2, c, :], bank[2 + u % 2][:, c * P:(c + 1) * P], ACT.Gelu_apprx_tanh,
                                         bias=w1_now[:, u % 2, HID + c:HID + c + 1]).then_inc(s_hid, 1)

            def slot(i, u):
                n, _, v = ahead(i, u, 2, 4)
                if exists(n, SLOTS):
                    xT_out(n, v)
                n, _, v = ahead(i, u, 1, 4)
                if exists(n, SLOTS):
                    hidden(n, v)

            xT_out(0, 0)
            xT_out(1, 1)
            hidden(0, 0)
            repeat(act, slot, SLOTS, 4)

            def finish(i, odd):
                g = i * 2 + odd
                act.wait_ge(s_nm4, g + 1)
                if exists(g - 2, G):
                    act.wait_ge(s_mul4, g - 1)
                for j in range(GT):
                    last = nc.scalar.activation(y[odd][:, j, :], acc[odd][:, j, :], ACT.Identity,
                                                scale=rstd4[:, odd, j:j + 1], bias=nm4[:, odd, j:j + 1])
                last.then_inc(s_norm4, 1)

            repeat(act, finish, G, 2)

        @block.vector
        def _(dve):
            dve.wait_ge(s_w, 16 * SMALL)
            wv_heads = wvg[:, 0, :].rearrange("p (h d) -> p h d", h=HEADS)
            nc.vector.tensor_reduce(vmean[:, :], wv_heads, AX_X, ALU.add).then_inc(s_w0, 1)
            dve.wait_ge(s_w0, 1)
            nc.vector.scalar_tensor_tensor(out=wv_heads, in0=vmean[:, :].unsqueeze(2).to_broadcast([P, HEADS, DH]),
                                           scalar=-1.0 / DH, in1=wv_heads, op0=ALU.mult, op1=ALU.add).then_inc(s_prep, 1)
            nc.vector.tensor_scalar(wo_s[:, :], wo_s[:, :], 0.5, None, ALU.mult).then_inc(s_prep, 1)
            nc.vector.tensor_copy(b2hi[:, :, :], b2_s[:, :, :]).then_inc(s_w0, 1)
            dve.wait_ge(s_w0, 2)
            nc.vector.tensor_tensor(b2rest[:, :, :], b2_s[:, :, :], b2hi[:, :, :], ALU.subtract).then_inc(s_w0, 1)
            dve.wait_ge(s_w0, 3)
            nc.vector.tensor_copy(b2mid[:, :, :], b2rest[:, :, :]).then_inc(s_w0, 1)
            dve.wait_ge(s_w0, 4)
            nc.vector.tensor_tensor(b2rest2[:, :, :], b2rest[:, :, :], b2mid[:, :, :], ALU.subtract).then_inc(s_w0, 1)
            dve.wait_ge(s_w0, 5)
            nc.vector.tensor_copy(b2lo[:, :, :], b2rest2[:, :, :]).then_inc(s_w0, 1)
            nc.vector.memset(ones3[:, :], 1.0).then_inc(s_prep, 1)
            dve.wait_ge(s_b1t, 1)
            nc.vector.tensor_copy(w1_s[:, :, HID:HID + HC], ps_a[:, 0:E * HC].rearrange("p (e c) -> p e c", c=HC)).then_inc(s_b1, 1)
            nc.vector.memset(ones[:, :], 1.0)
            nc.vector.memset(before[:, :], 0.0)
            nc.vector.memset(zrow[:, 0:D], 0.0).then_inc(s_zrow, 1)
            nc.vector.memset(zrow[:, D:XW], float(PAIRS)).then_inc(s_zrow, 1)
            for choice in range(2):
                nc.vector.memset(xrow[:, choice, :, D + 1], float(choice))

            dve.wait_ge(s_x0, 32)
            dve.wait_ge(s_cst, 16)
            nc.vector.tensor_copy(earlier[:, :], cst[:, C_EARLIER:C_EARLIER + P]).then_inc(s_prep, 1)
            nc.vector.tensor_scalar(xrow[:, :, :, D], cst[:, C_TOKEN:C_TOKEN + GT].unsqueeze(1).to_broadcast([P, 2, GT]),
                                    -2.0 * GN, None, ALU.add)
            steps = 0

            def chain(instruction):
                nonlocal steps
                steps += 1
                instruction.then_inc(s_top, 1)
                dve.wait_ge(s_top, steps)

            def scores(chunks):
                for c in chunks:
                    half = c // NCH
                    dve.wait_ge(s_x[c % RING], 16 * (c // RING + 1))
                    for t in range(CH):
                        n = c % NCH * CH + t
                        row = xring[:, c % RING, t * D:(t + 1) * D]
                        last = nc.vector.tensor_tensor_reduce(
                            out=row, in0=row, in1=tokw[:, :],
                            scale=1.0, scalar=0.0, op0=ALU.mult, op1=ALU.add, accum_out=score[:, half, n:n + 1])
                    last.then_inc(s_score, 1)

            def select(half):
                scored(dve, half)
                sc = score[:, half, :]
                chain(nc.vector.tensor_scalar(sc, sc, tokb[:, 0:1], None, ALU.add))
                chain(nc.vector.max(best[:, 0:8], sc))
                chain(nc.vector.max_index(besti[:, 0:8], best[:, 0:8], sc))
                chain(nc.vector.match_replace(score2[:, :], best[:, 0:8], sc, LOWEST))
                chain(nc.vector.max(best[:, 8:16], score2[:, :]))
                chain(nc.vector.max_index(besti[:, 8:16], best[:, 8:16], score2[:, :]))
                chain(nc.vector.tensor_scalar(bestf[:, :], besti[:, :], cst[:, C_BASE:C_BASE + 1], float(half * P * BLOCK),
                                              ALU.add, ALU.add))
                nc.vector.tensor_tensor(spread[:, :, :], bestf[:, :].unsqueeze(1).to_broadcast([P, 8, TOPK]),
                                        cst[:, C_ROW8:C_ROW8 + 8].unsqueeze(2).to_broadcast([P, 8, TOPK]),
                                        ALU.mult).then_inc(s_spread, 1)
                dve.wait_ge(s_idxps, half + 1)
                nc.vector.tensor_copy(index[:, half * 16:half * 16 + 16], ps_c[:, 0:16]).then_inc(s_index, 1)

            def statistics(stats_, meanvar_, rows):
                for j in range(GT):
                    nc.vector.bn_stats(stats_[:, j, :], rows[j])
                dve.drain()
                for j in range(GT):
                    nc.vector.bn_aggr(meanvar_[:, j, :], stats_[:, j, :])
                dve.drain()

            def hsel_g(g, j):
                return hsel[:, ds(g * GT + j, 1), :].rearrange("p a d -> p (a d)")

            def minus_mean(dst, meanvar_, rstd):
                return nc.vector.scalar_tensor_tensor(out=dst, in0=meanvar_[:, :, 0], scalar=-1.0, in1=rstd,
                                                      op0=ALU.mult, op1=ALU.mult)

            def probs(g, r):
                dve.wait_ge(s_sc, g * 2 + r + 1)
                for t in (2 * r, 2 * r + 1):
                    nc.vector.tensor_tensor(prob[:, t, :, :].rearrange("p (j i) n -> p j (i n)", i=2), pscore[:, :, t % 2, :],
                                            decay, ALU.mult).then_inc(s_prob, 1)

            def step(i):
                if here(i):
                    probs(i, 0)
                if here(i - 3):
                    dve.wait_ge(s_r, i - 2)
                    nc.vector.tensor_copy(logit[:, :, :], ps_a[:, 0:GT * E].rearrange("p (t e) -> p t e", e=E)).then_inc(s_logit, 1)
                    dve.drain()
                    for j in range(GT):
                        nc.vector.max(topg[:, j, :], logit[:, j, :])
                    dve.drain()
                    for j in range(GT):
                        nc.vector.max_index(topig[:, j, :], topg[:, j, :], logit[:, j, :])
                    nc.vector.tensor_copy(top12[:, ds((i - 3) * GT, GT), :], topg[:, :, 0:2]).then_inc(s_tc, 1)
                    dve.drain()
                    nc.vector.tensor_copy(topf[:, :, :], topig[:, :, 0:2].rearrange("p t k -> p k t"))
                    dve.drain()
                    nc.vector.tensor_tensor(pick[:, :, :, :].rearrange("p k t e -> p (k t) e"),
                                            cst[:, C_IOTA:C_IOTA + E].unsqueeze(1).to_broadcast([P, 2 * GT, E]),
                                            topf[:, :, :].rearrange("p k t -> p (k t)").unsqueeze(2).to_broadcast([P, 2 * GT, E]),
                                            ALU.is_equal)
                    dve.drain()
                    nc.vector.tensor_tensor(chosen[:, :, :], pick[:, 0], pick[:, 1], ALU.add).then_inc(s_pick, 1)
                    if here(i - 4):
                        dve.wait_ge(s_scat, (i - 3) * 2 * GT * 16)
                    nc.vector.tensor_copy(xrow[:, :, :, 0:D], xhat[:, :, :].unsqueeze(1).to_broadcast([P, 2, GT, D])).then_inc(s_row, 1)
                    nc.vector.tensor_scalar(xrow[:, :, :, D], xrow[:, :, :, D], 2.0 * GN, None, ALU.add)
                    dve.drain()
                    nc.vector.tensor_reduce(chosen_sum[:, :], chosen[:, :, :].rearrange("p t e -> p e t"), AX_X, ALU.add)
                    dve.wait_ge(s_rank, i - 2)
                    nc.vector.tensor_tensor(rank[:, :, :], ps_c[:, 0:GT * E].rearrange("p (t e) -> p t e", e=E),
                                            cst[:, C_REGION:C_REGION + E].unsqueeze(1).to_broadcast([P, GT, E]),
                                            ALU.add).then_inc(s_rankc, 1)
                    dve.drain()
                    nc.vector.tensor_tensor(before[:, :], before[:, :], chosen_sum[:, :], ALU.add).then_inc(s_rankc, 1)
                    nc.vector.tensor_tensor(rank_pick[:, :, :, :], pick[:, :, :, :],
                                            rank[:, :, :].unsqueeze(1).to_broadcast([P, 2, GT, E]), ALU.mult)
                    dve.drain()
                    nc.vector.tensor_reduce(posf[:, :, :], rank_pick[:, :, :, :], AX_X, ALU.add)
                    dve.drain()
                    nc.vector.tensor_copy(pos[:, :], posf[:, :, :].rearrange("p k t -> p (k t)")).then_inc(s_pos, 1)
                if isinstance(i, int) and i in (0, 1):
                    mine = chunks_of(1, 0)
                    scores(mine[:3] if i == 0 else mine[3:])
                    if i == 1:
                        select(1)
                if here(i - 2):
                    dve.wait_ge(s_wo, i - 1)
                    tiles = hsel[:, ds((i - 2) * GT, GT), :]
                    nc.vector.tensor_tensor(tiles, ps_c[:, :].rearrange("p (t d) -> p t d", t=GT), tiles, ALU.add)
                    dve.drain()
                    statistics(stats[:, 1], meanvar2, [hsel_g(i - 2, j) for j in range(GT)])
                    if here(i - 3):
                        dve.wait_ge(s_hn2, (i - 2) * GT)
                    nc.vector.tensor_scalar(var2[:, :], meanvar2[:, :, 1], EPS, None, ALU.add).then_inc(s_stat2, 1)
                    nc.vector.tensor_scalar(var3[:, :], meanvar2[:, :, 1], 1.0 + EPS, EPS * EPS,
                                            ALU.mult, ALU.add).then_inc(s_stat2, 1)
                if here(i - 1):
                    dve.wait_ge(s_sq, i)
                    nc.vector.tensor_reduce(gvar[:, :], square[:, :].rearrange("p (a d) -> p a d", d=DH), AX_X, ALU.add)
                    dve.drain()
                    nc.vector.tensor_scalar(gvar2[:, :], gvar[:, :], 1.0 / DH, EPS, ALU.mult, ALU.add).then_inc(s_gvar, 1)
                if here(i - 2):
                    dve.wait_ge(s_rs2, (i - 2) * 2 + 2)
                    minus_mean(nm2[:, :], meanvar2, rstd2[:, :]).then_inc(s_nm2, 1)
                    minus_mean(nm3[:, :], meanvar2, rstd3[:, :]).then_inc(s_nm2, 1)
                if here(i):
                    probs(i, 1)
                if here(i - 1):
                    dve.wait_ge(s_grs, i)
                    nc.vector.tensor_tensor(normed[:, :, :].rearrange("p t (h d) -> p (t h) d", d=DH),
                                            ps_a[:, :].rearrange("p (a d) -> p a d", d=DH),
                                            grstd[:, :].unsqueeze(2).to_broadcast([P, GT * HEADS, DH]), ALU.mult).then_inc(s_norm, 1)
                if here(i + 2):
                    if isinstance(i, int):
                        dve.wait_ge(s_gather[i + 2], 16 * GT)
                    else:
                        dve.wait_ge(s_gather[G - 1], 16 * GT)
                    statistics(stats[:, 0], meanvar, [hsel_g(i + 2, j) for j in range(GT)])
                    if here(i + 1):
                        dve.wait_ge(s_ln, i + 2)
                    nc.vector.tensor_scalar(var1[:, :], meanvar[:, :, 1], EPS, None, ALU.add).then_inc(s_stat1, 1)
                    dve.wait_ge(s_rs1, i + 3)
                    minus_mean(nm1[:, :], meanvar, rstd1[:, :]).then_inc(s_nm1, 1)
                if here(i - 1):
                    dve.wait_ge(s_th, i)
                    nc.vector.scalar_tensor_tensor(out=act_s[:, :, :], in0=th[:, :, :], scalar=1.0, in1=pre[:, :, :],
                                                   op0=ALU.add, op1=ALU.mult).then_inc(s_act, 1)

            scores(chunks_of(0, 0))
            select(0)
            mix_schedule(dve, step)

            done = 0

            def seq(instruction):
                nonlocal done
                done += 1
                instruction.then_inc(s_slot, 1)
                dve.wait_ge(s_slot, done)

            dve.wait_ge(s_cnt, 1)
            seq(nc.vector.tensor_copy(count[:, :], ps_b[:, 0:E]))
            nc.vector.tensor_tensor(padpos[:, :], count[:, :], cst[:, C_PAD:C_PAD + E], ALU.add).then_inc(s_cnt, 1)
            seq(nc.vector.tensor_tensor(reached[:, :, :], count[:, :].unsqueeze(2).to_broadcast([P, E, TILES]),
                                        cst[:, C_TILE:C_TILE + TILES].unsqueeze(1).to_broadcast([P, E, TILES]), ALU.is_gt))
            seq(nc.vector.tensor_reduce(ntiles[:, :], reached[:, :, :], AX_X, ALU.add))
            seq(nc.vector.tensor_tensor(tri[:, :, :], ntiles[:, :].unsqueeze(1).to_broadcast([P, E, E]),
                                        cst[:, C_TRI8:C_TRI8 + E * E].rearrange("p (a b) -> p a b", b=E), ALU.mult))
            seq(nc.vector.tensor_reduce(ends[:, :], tri[:, :, :], AX_X, ALU.add))
            seq(nc.vector.tensor_scalar(passed[:, :], ends[:, :], cst[:, C_SLOT:C_SLOT + 1], None, ALU.is_le))
            seq(nc.vector.tensor_scalar(jump[:, :], ntiles[:, :], -float(P), float(REGION), ALU.mult, ALU.add))
            seq(nc.vector.tensor_tensor(jumps[:, :], jump[:, :], passed[:, :], ALU.mult))
            seq(nc.vector.tensor_reduce(slot_row[:, :], jumps[:, 0:E - 1], AX_X, ALU.add))
            seq(nc.vector.tensor_reduce(slot_e[:, :], passed[:, 0:E - 1], AX_X, ALU.add))
            seq(nc.vector.tensor_scalar(slot_row[:, :], slot_row[:, :], cst[:, C_BASE:C_BASE + 1], -float(E * REGION),
                                        ALU.add, ALU.add))
            seq(nc.vector.tensor_scalar(slot_in[:, :], passed[:, E - 1:E], -1.0, 1.0, ALU.mult, ALU.add))
            seq(nc.vector.tensor_tensor(slot_row[:, :], slot_row[:, :], slot_in[:, :], ALU.mult))
            nc.vector.tensor_scalar(slot_cols[:, 0:1], slot_row[:, :], float(E * REGION), None, ALU.add).then_inc(s_tab, 1)
            nc.vector.tensor_copy(slot_cols[:, 1:2], slot_e[:, :]).then_inc(s_tab, 1)
            dve.wait_ge(s_tab, 3)
            nc.vector.tensor_copy(table[:, :], ps_c[0:1, 0:2 * P]).then_inc(s_tabT, 1)

            dve.wait_ge(s_tc, G)
            nc.vector.tensor_tensor(gap[:, :], top12[:, :, 1], top12[:, :, 0], ALU.subtract).then_inc(s_rt, 1)
            dve.wait_ge(s_e2, 1)
            nc.vector.tensor_scalar(esum[:, :], e2[:, :], 1.0, None, ALU.add).then_inc(s_rt, 1)
            dve.wait_ge(s_rt, 2)
            nc.vector.reciprocal(conf12[:, :, 0], esum[:, :]).then_inc(s_rt, 1)
            dve.wait_ge(s_rt, 3)
            nc.vector.tensor_tensor(conf12[:, :, 1], conf12[:, :, 0], e2[:, :], ALU.mult).then_inc(s_rt, 1)
            dve.wait_ge(s_rt, 4)
            dve.wait_ge(s_hn2, TILES)
            for g in range(G):
                tiles = hsel[:, g * GT:(g + 1) * GT, :]
                nc.vector.tensor_tensor(tiles, tiles, outb[:, :].unsqueeze(1).to_broadcast([P, GT, D]),
                                        ALU.add).then_inc(s_hb, 1)
            dve.wait_ge(s_hb, G)

            def first_weights(n, u):
                e = dve.value_load(table[0:1, ds(n + P, 1)], min_val=0, max_val=E - 1)
                nc.vector.tensor_copy(w1_now[:, u % 2, :], w1_s[:, ds(e, 1), :].rearrange("p a b -> p (a b)")).then_inc(s_w1, 1)

            def slot(i, u):
                s = i * 4 + u
                if exists(s - 4, SLOTS):
                    dve.wait_ge(s_pairs[u], i * 16)
                n, _, v = ahead(i, u, 2, 4)
                if exists(n, SLOTS):
                    dve.wait_ge(s_hid, (s + 1) * HC)
                dve.wait_ge(s_xin[u], (i + 1) * 16)
                nc.vector.tensor_copy(ids[:, u, :], xin[:, u, D:XW]).then_inc(s_ids, 1)
                if exists(n, SLOTS):
                    first_weights(n, v)
                dve.wait_ge(s_down, s + 1)
                nc.vector.tensor_copy(yslot[:, u, :], down[u % 2][:, 0:D]).then_inc(s_y, 1)

            dve.wait_ge(s_wbig, 16 * 2 * E)
            first_weights(0, 0)
            first_weights(1, 1)
            repeat(dve, slot, SLOTS, 4)

            def sum_up(n, i, odd):
                dve.wait_ge(s_load[odd], (i + 1) * 16)
                if exists(n - 2, G):
                    dve.wait_ge(s_norm4, n - 1)
                for k, (src, dst) in enumerate(((None, acc1[odd]), (acc1[odd], acc[odd]))):
                    for j in range(GT):
                        tile = n * GT + j
                        before_ = src[:, j, :] if k else hn2[:, ds(tile, 1), :].rearrange("p a d -> p (a d)")
                        nc.vector.scalar_tensor_tensor(
                            out=dst[:, j, :], in0=ypair[:, ds(n, 1), j, k, :].rearrange("p a d -> p (a d)"),
                            scalar=conf12[:, ds(tile, 1), k:k + 1].rearrange("p a b -> p (a b)"), in1=before_,
                            op0=ALU.mult, op1=ALU.add)
                    dve.drain()

            def spread_of(n, odd):
                statistics(stats3, meanvar3[odd], [acc[odd][:, j, :] for j in range(GT)])
                nc.vector.tensor_scalar(var4[:, odd, :], meanvar3[odd][:, :, 1], EPS, None, ALU.add).then_inc(s_stat3, 1)

            def finish(i, odd):
                g = i * 2 + odd
                n, ni, v = ahead(i, odd, 1, 2)
                if exists(n, G):
                    sum_up(n, ni, v)
                dve.wait_ge(s_rs4, g + 1)
                minus_mean(nm4[:, odd, :], meanvar3[odd], rstd4[:, odd, :]).then_inc(s_nm4, 1)
                if exists(n, G):
                    spread_of(n, v)
                dve.wait_ge(s_mul4, g + 1)
                if exists(g - 2, G):
                    dve.wait_ge(s_out[odd], i * 16)
                nc.vector.tensor_tensor(yo[:, odd, :, :], yw[odd][:, :, :], hsel[:, ds(g * GT, GT), :],
                                        ALU.add).then_inc(s_fin, 1)

            sum_up(0, 0, 0)
            spread_of(0, 0)
            repeat(dve, finish, G, 2)

        @block.tensor
        def _(pe):
            pe.wait_ge(s_w, 16 * SMALL)
            pe.wait_ge(s_cst, 16)
            pe.transpose(ps_a[:, 0:E * HC], b1_rows[:, :], ident[0:E * HC, 0:E * HC]).then_inc(s_b1t, 1)

            def index_turn(half):
                pe.wait_ge(s_spread, half + 1)
                pe.matmul(ps_c[:, 0:16], spread[:, :, :].rearrange("p a b -> p (a b)"), cst[:, C_ROW16:C_ROW16 + 16],
                          start=True, stop=True).then_inc(s_idxps, 1)

            def turn(dst, src, done):
                for j in range(GT):
                    last = pe.transpose(dst[:, j * P:(j + 1) * P], src[:, j, :], ident)
                last.then_inc(done, 1)

            def scores(g, r):
                for t in (2 * r, 2 * r + 1):
                    for j in range(4):
                        last = pe.matmul(pscore[:, j, t % 2, :], kT[32 * j:32 * j + 32, t * P:(t + 1) * P],
                                         qeo[32 * j:32 * j + 32, t, :, :].rearrange("p i n -> p (i n)"),
                                         start=True, stop=True)
                last.then_inc(s_sc, 1)

            def retention(g, r):
                pe.wait_ge(s_prob, g * GT + 2 * r + 2)
                for t in (2 * r, 2 * r + 1):
                    for j in range(4):
                        for odd in range(2):
                            last = pe.matmul(ps_ret[32 * j:32 * j + 32, t * P:(t + 1) * P], vpad[:, t, odd, 32 * j:32 * j + 32],
                                             prob[:, t, 2 * j + odd, :], start=(odd == 0), stop=(odd == 1))
                if r == 1:
                    last.then_inc(s_ret, 1)

            def step(i):
                if here(i):
                    pe.wait_ge(s_kc, i + 1)
                    pe.wait_ge(s_qc, i * 2 + 2)
                    if here(i - 1):
                        pe.wait_ge(s_prob, i * GT)
                    scores(i, 0)
                if here(i - 2):
                    pe.wait_ge(s_act, i - 1)
                    turn(ps_b, act_s, s_tz)
                if here(i - 1):
                    retention(i - 1, 1)
                if here(i):
                    if here(i - 2):
                        pe.wait_ge(s_norm, i - 1)
                    if here(i - 3):
                        pe.wait_ge(s_logit, i - 2)
                    for j in range(GT):
                        last = pe.matmul(ps_a[:, j * D:(j + 1) * D], lnT[:, j * P:(j + 1) * P], wvg[:, 0, :], start=True, stop=True)
                    last.then_inc(s_v, 1)
                    if here(i - 2):
                        pe.wait_ge(s_zT, i - 1)
                    for j in range(GT):
                        last = pe.matmul(ps_b[:, j * D:(j + 1) * D], lnT[:, j * P:(j + 1) * P], wvg[:, 1, :], start=True, stop=True)
                    last.then_inc(s_g, 1)
                if here(i - 3):
                    pe.wait_ge(s_pick, i - 2)
                    if here(i + 0):
                        pe.wait_ge(s_qc, i * 2 + 2)
                    if here(i - 4):
                        pe.wait_ge(s_rankc, (i - 3) * 2)
                    seen = ps_c[:, 0:GT * E].rearrange("p (t e) -> p t e", e=E)
                    pe.matmul(seen, earlier[:, :], chosen[:, :, :], start=True, stop=False)
                    for t in range(GT - 1):
                        pe.matmul(seen[:, t + 1:GT, :], ones[:, :], chosen[:, t:t + 1, :].to_broadcast([P, GT - 1 - t, E]),
                                  start=False, stop=False)
                    pe.matmul(seen, ones[:, :], before[:, :].unsqueeze(1).to_broadcast([P, GT, E]),
                              start=False, stop=True).then_inc(s_rank, 1)
                if here(i - 2):
                    pe.wait_ge(s_zT, i - 1)
                    if here(i - 3):
                        pe.wait_ge(s_rankc, (i - 2) * 2)
                    for j in range(GT):
                        last = pe.matmul(ps_c[:, j * D:(j + 1) * D], actT[:, j * P:(j + 1) * P], wo_s[:, :], start=True, stop=True)
                    last.then_inc(s_wo, 1)
                if here(i - 1):
                    pe.wait_ge(s_retc, i)
                    if here(i):
                        pe.wait_ge(s_vc, i * 2 + 2)
                    if here(i - 3):
                        pe.wait_ge(s_logit, i - 2)
                    turn(ps_a, retT, s_tret)
                if here(i + 1):
                    pe.wait_ge(s_ln, i + 2)
                    if here(i):
                        pe.wait_ge(s_gc, i + 1)
                    turn(ps_b, ln, s_t1)
                if here(i):
                    pe.wait_ge(s_prob, i * GT + 2)
                    scores(i, 1)
                if isinstance(i, int) and i == 1:
                    index_turn(1)
                if here(i - 2):
                    pe.wait_ge(s_xhat, i - 1)
                    turn(ps_c, xhat, s_t3)
                if here(i + 1):
                    pe.wait_ge(s_lnT, i + 2)
                    pe.matmul(ps_b[:, :], wk_s[:, :], lnT[:, :], start=True, stop=True).then_inc(s_k, 1)
                    if isinstance(i, int) and i == 1:
                        pe.wait_ge(s_index, 2)
                    if here(i - 2):
                        pe.wait_ge(s_xnT, i - 1)
                    pe.matmul(ps_c[:, :], wq_s[:, :], lnT[:, :], start=True, stop=True).then_inc(s_q, 1)
                if here(i):
                    if here(i - 1):
                        pe.wait_ge(s_retc, i)
                    pe.wait_ge(s_vc, i * 2 + 2)
                    retention(i, 0)
                if here(i - 2):
                    pe.wait_ge(s_xnT, i - 1)
                    if here(i - 1):
                        pe.wait_ge(s_norm, i)
                    for j in range(GT):
                        last = pe.matmul(ps_a[:, j * E:(j + 1) * E], xnTg[:, j * P:(j + 1) * P], wgate[:, :], start=True, stop=True)
                    last.then_inc(s_r, 1)

            index_turn(0)
            pe.wait_ge(s_b1, 1)
            pe.wait_ge(s_prep, 4)
            pe.wait_ge(s_index, 1)
            mix_schedule(pe, step)
            pe.wait_ge(s_rankc, 2 * G)
            pe.matmul(ps_b[:, 0:E], ones[:, :], before[:, :], start=True, stop=True).then_inc(s_cnt, 1)
            pe.wait_ge(s_tab, 2)
            for k in range(2):
                last = pe.matmul(ps_c[0:1, k * P:(k + 1) * P], slot_cols[:, k:k + 1], ident, start=True, stop=True)
            last.then_inc(s_tab, 1)
            pe.wait_ge(s_wbig, 16 * 2 * E)
            pe.wait_ge(s_parts, 48)
            pe.wait_ge(s_tabT, 1)

            def turn_slot(n, i, u):
                pe.wait_ge(s_xin[u], (i + 1) * 16)
                if exists(n - 2, SLOTS):
                    pe.wait_ge(s_xTc, n - 1)
                pe.transpose(bank[u % 2][:, 0:P], xin[:, u, 0:D], ident).then_inc(s_xt, 1)

            def up(n, u):
                pe.wait_ge(s_xTc, n + 1)
                pe.wait_ge(s_w1, n + 1)
                if exists(n - 2, SLOTS):
                    pe.wait_ge(s_hid, (n - 1) * HC)
                for c in range(HC):
                    last = pe.matmul(bank[2 + u % 2][:, c * P:(c + 1) * P], w1_now[:, u % 2, c * P:(c + 1) * P], xT[:, u % 2, :],
                                     start=True, stop=True)
                last.then_inc(s_up, 1)

            def lower(n, u):
                e = pe.value_load(table[0:1, ds(n + P, 1)], min_val=0, max_val=E - 1)
                pe.wait_ge(s_hid, (n + 1) * HC)
                if exists(n - 2, SLOTS):
                    pe.wait_ge(s_y, n - 1)
                dst = down[u % 2][:, 0:D]
                pe.matmul(dst, ones3[:, :], b2_parts[:, ds(e, 1), :].rearrange("p a d -> p (a d)"), start=True, stop=False)
                for c in range(HC):
                    last = pe.matmul(dst, hid[:, u % 2, c, :], w2_s[:, ds(e, 1), c, :].rearrange("p a d -> p (a d)"),
                                     start=False, stop=(c == HC - 1))
                last.then_inc(s_down, 1)

            def slot(i, u):
                n, ni, v = ahead(i, u, 2, 4)
                if exists(n, SLOTS):
                    turn_slot(n, ni, v)
                n, ni, v = ahead(i, u, 1, 4)
                if exists(n, SLOTS):
                    up(n, v)
                lower(i * 4 + u, u)

            turn_slot(0, 0, 0)
            turn_slot(1, 0, 1)
            up(0, 0)
            repeat(pe, slot, SLOTS, 4)


_INS = ["x", "L0_tok_W", "L0_tok_b", "L0_attn_W_Q", "L0_attn_W_K", "L0_attn_W_V", "L0_attn_W_G", "L0_attn_W_O",
        "L0_attn_gn_weight", "L0_attn_gn_bias", "L0_ffn_Wg", "L0_ffn_W1", "L0_ffn_b1", "L0_ffn_W2", "L0_ffn_b2",
        "L0_ffn_ln_g", "L0_ffn_ln_b", "L0_ffn_out_g", "L0_ffn_out_b"]


def kernel(**inputs):
    import concourse.bacc as bacc
    from concourse.bass_utils import run_bass_kernel_spmd

    nc = bacc.Bacc("TRN2", target_bir_lowering=False, num_devices=1)
    arrays = {name: np.ascontiguousarray(inputs[name]) for name in _INS}
    arrays["consts"] = constants()
    args = [nc.dram_tensor(name, a.shape, mybir.dt.from_np(a.dtype), kind="ExternalInput").ap()
            for name, a in arrays.items()]
    out = nc.dram_tensor("out", (B, T, D), F32, kind="ExternalOutput").ap()
    routed = nc.dram_tensor("routed", (E * REGION + P, XW), F32, kind="Internal").ap()
    pairs = nc.dram_tensor("pairs", (PAIRS, D), F32, kind="Internal").ap()
    program(nc, *args, out, routed, pairs)
    return run_bass_kernel_spmd(nc, [arrays], core_ids=[0]).results[0]["out"]
```

```python
from contextlib import ExitStack

import numpy as np

import concourse.bass as bass
from concourse import mybir

ALU = mybir.AluOpType
ACT = mybir.ActivationFunctionType
F32 = mybir.dt.float32
BF16 = mybir.dt.bfloat16
U32 = mybir.dt.uint32
I32 = mybir.dt.int32
AX_X = mybir.AxisListType.X

P = 128
B, S, D = 128, 256, 128
BLOCK, TOPK = 128, 16
ROWS = B * S // BLOCK
HALVES = ROWS // P
T = S // BLOCK * TOPK
TILES = B * T // P
GT = 4
GN = GT * P
G = TILES // GT
HEADS, DH = 8, 16
E, HID = 8, 512
HC = HID // P
EPS = 1e-5
REGION = TILES * P + P
PAIRS = 2 * TILES * P
SLOTS = 2 * TILES + E - 1
XW = D + 2
LOWEST = -3.4028234663852886e38
CH = 16
NCH = BLOCK // CH
RING = 5
C_MASK, C_ID = 0, HEADS * P
C_PAR = C_ID + P
C_ROW8 = C_PAR + 2
C_ROW16 = C_ROW8 + 8
C_BASE = C_ROW16 + 16
C_IOTA = C_BASE + 1
C_REGION = C_IOTA + E
C_TOKEN = C_REGION + E
C_TRI8 = C_TOKEN + GT
C_TILE = C_TRI8 + E * E
C_SLOT = C_TILE + TILES
C_EARLIER = C_SLOT + 1
C_ALL = C_EARLIER + P


def constants():
    c = np.zeros((P, C_ALL), np.float32)
    p = np.arange(P)
    s, t = p[:, None], p[None, :]
    seen = (s // T == t // T) & (t >= s)
    for h in range(HEADS):
        gamma = 1.0 - 2.0 ** (-5.0 - h)
        c[:, C_MASK + h * P:C_MASK + (h + 1) * P] = np.where(seen, gamma ** np.maximum(t - s, 0), 0.0)
    c[:, C_ID:C_ID + P] = np.eye(P)
    c[:, C_PAR] = DH ** -0.5 * (p // DH % 2 == 0)
    c[:, C_PAR + 1] = DH ** -0.5 * (p // DH % 2 == 1)
    c[:, C_ROW8:C_ROW8 + 8] = p[:, None] % 8 == np.arange(8)
    c[:, C_ROW16:C_ROW16 + 16] = p[:, None] // 8 == np.arange(16)
    c[:, C_BASE] = BLOCK * p
    c[:, C_IOTA:C_IOTA + E] = np.arange(E)
    c[:, C_REGION:C_REGION + E] = REGION * np.arange(E)
    c[:, C_TOKEN:C_TOKEN + GT] = 2 * (P * np.arange(GT) + s)
    c[:, C_TRI8:C_TRI8 + E * E] = (np.arange(E)[None, :] <= np.arange(E)[:, None]).reshape(-1)
    c[:, C_TILE:C_TILE + TILES] = P * np.arange(TILES)
    c[:, C_SLOT] = p
    c[:, C_EARLIER:C_EARLIER + P] = s < t
    return c


ds = bass.ds
SMALL = 14


def program(nc, x, tok_w, tok_b, wq, wk, wv, wg, wo, gn_w, gn_b, ffn_wg, w1, b1, w2, b2,
            ln_g, ln_b, out_g, out_b, consts, out, routed, pairs, bias_rows):
    x_chunks = x.rearrange("b (k c t) d -> (b k) c (t d)", c=NCH, t=CH)
    x_tokens = x.rearrange("b s d -> (b s) d")
    out_groups = out.rearrange("b t d -> (b t) d").rearrange("(g j p) d -> g p j d", j=GT, p=P)

    pair_groups = pairs.rearrange("(g j p k) d -> g p j k d", j=GT, p=P, k=2)

    with ExitStack() as ctx:
        def sb(name, shape, dt=F32):
            return ctx.enter_context(nc.sbuf_tensor(name, shape, dt))

        def ps(name, shape):
            return ctx.enter_context(nc.psum_tensor(name, shape, F32))

        def sem(name):
            return ctx.enter_context(nc.semaphore(name))

        cst = sb("cst", [P, C_ALL])
        decay = cst[:, C_MASK:C_MASK + HEADS * P].rearrange("p (j n) -> p j n", j=4)
        ident = cst[:, C_ID:C_ID + P]
        tokw = sb("tokw", [P, D])
        tokb = sb("tokb", [P, 1])
        wq_s, wk_s, wo_s = sb("wq_s", [P, D]), sb("wk_s", [P, D]), sb("wo_s", [P, D])
        wvg = sb("wvg", [P, 2, D])
        vmean = sb("vmean", [P, HEADS])
        gnw = sb("gnw", [P, D])
        outg, outb = sb("outg", [P, D]), sb("outb", [P, D])
        lng, lnb = sb("lng", [P, 1]), sb("lnb", [P, 1])
        wgate = sb("wgate", [P, E])
        w1_s = sb("w1_s", [P, E, HID + HC])
        w2_s = sb("w2_s", [P, E, HC, D])
        b1_rows = sb("b1_rows", [E * HC, P])
        xring = sb("xring", [P, RING, CH * D])
        score = sb("score", [P, HALVES, BLOCK])
        score2 = sb("score2", [P, BLOCK])
        best = sb("best", [P, TOPK])
        besti = sb("besti", [P, TOPK], U32)
        bestf = sb("bestf", [P, TOPK])
        spread = sb("spread", [P, 8, TOPK])
        index = sb("index", [P, TILES], U32)
        hsel = sb("hsel", [P, TILES, D])
        stats = sb("stats", [P, 2, GT, 6])
        meanvar = sb("meanvar", [P, GT, 2])
        meanvar2 = sb("meanvar2", [P, GT, 2])
        var1 = sb("var1", [P, GT])
        rstd1, nm1 = sb("rstd1", [P, GT]), sb("nm1", [P, GT])
        ln = sb("ln", [P, GT, D])
        lnT = sb("lnT", [P, GN])
        qeo = sb("qeo", [P, GT, 2, P])
        kT = sb("kT", [P, GN])
        vpad = sb("vpad", [P, GT, 2, D])
        retT = sb("retT", [P, GT, P])
        prob = sb("prob", [P, GT, HEADS, P])
        square = sb("square", [P, GN])
        gvar = sb("gvar", [P, GT * HEADS])
        gvar2, grstd = sb("gvar2", [P, GT * HEADS]), sb("grstd", [P, GT * HEADS])
        root_a, root_b = sb("root_a", [P, GT * HEADS]), sb("root_b", [P, GT * HEADS])
        var23, rstd23, nm23 = sb("var23", [P, 2, GT]), sb("rstd23", [P, 2, GT]), sb("nm23", [P, 2, GT])
        minus2 = sb("minus2", [P, GT])
        var2, var3, rstd2, rstd3, nm2, nm3 = (m[:, n] for m in (var23, rstd23, nm23) for n in range(2))
        halves = sb("halves", [P, 2 * GT])
        gate = sb("gate", [P, GT, D])
        normed = sb("normed", [P, GT, D])
        normw = sb("normw", [P, GT, D])
        pre = sb("pre", [P, GT, D])
        th = sb("th", [P, GT, D])
        act_s = sb("act_s", [P, GT, D])
        actT = sb("actT", [P, GN])
        var4, rstd4 = sb("var4", [P, 2, GT]), sb("rstd4", [P, 2, GT])
        xnTg = sb("xnTg", [P, GN])
        topg, topig = sb("topg", [P, GT, 8]), sb("topig", [P, GT, 8], U32)
        hn2 = sb("hn2", [P, TILES, D])
        xhat = sb("xhat", [P, GT, D])
        logit = sb("logit", [P, GT, E])
        top12 = sb("top12", [P, TILES, 2])
        gap = sb("gap", [P, TILES])
        e2 = sb("e2", [P, TILES])
        esum = sb("esum", [P, TILES])
        conf12 = sb("conf12", [P, TILES, 2])
        topf = sb("topf", [P, 2, GT])
        pick = sb("pick", [P, 2, GT, E])
        chosen = sb("chosen", [P, GT, E], BF16)
        chosen_sum = sb("chosen_sum", [P, E])
        before = sb("before", [P, E], BF16)
        earlier, ones = sb("earlier", [P, P], BF16), sb("ones", [P, P], BF16)
        rank = sb("rank", [P, GT, E])
        rank_pick = sb("rank_pick", [P, 2, GT, E])
        posf = sb("posf", [P, 2, GT])
        pos = sb("pos", [P, 2 * GT], U32)
        xrow = sb("xrow", [P, 2, GT, XW])
        zrow = sb("zrow", [P, XW])
        count = sb("count", [P, E])
        rowend = sb("rowend", [P, E], I32)
        reached, ntiles = sb("reached", [P, E, TILES]), sb("ntiles", [P, E])
        tri, ends = sb("tri", [P, E, E]), sb("ends", [P, E])
        passed, jump, jumps = sb("passed", [P, E]), sb("jump", [P, E]), sb("jumps", [P, E])
        slot_row, slot_e, slot_in = sb("slot_row", [P, 1]), sb("slot_e", [P, 1]), sb("slot_in", [P, 1])
        slot_cols = sb("slot_cols", [P, 2])
        table = sb("table", [1, 2 * P], I32)
        xin = sb("xin", [P, 4, XW])
        ids, dest = sb("ids", [P, 4, 2], U32), sb("dest", [P, 4], U32)
        xT = sb("xT", [P, 2, P])
        w1_now = sb("w1_now", [P, 2, HID + HC])
        hid = sb("hid", [P, 2, HC, P])
        yslot = sb("yslot", [P, 4, D])
        ypair = xring[:, :, :].rearrange("p a b -> p (a b)")[:, 0:G * GT * 2 * D].rearrange(
            "p (g t k d) -> p g t k d", g=G, t=GT, k=2)
        bias = sb("bias", [E + 1, D])
        bias_hi, bias_mid, bias_lo = sb("bias_hi", [E + 1, D], BF16), sb("bias_mid", [E + 1, D], BF16), sb("bias_lo", [E + 1, D], BF16)
        bias_rest, bias_rest2 = sb("bias_rest", [E + 1, D]), sb("bias_rest2", [E + 1, D])
        bias_parts = sb("bias_parts", [3, E + 1, D], BF16)
        ones3 = sb("ones3", [3, P], BF16)
        yfin = sb("yfin", [P, GT, D])
        weighed1, weighed2, both = [th, retT], [xhat, yfin], [lnT, actT]
        acc, y, yw = [ln, normed], [act_s, pre], [normw, gate]
        both = [m[:, :].rearrange("p (t d) -> p t d", t=GT) for m in both]
        nm4 = sb("nm4", [P, 2, GT])
        yo = prob[:, 0].rearrange("p (a t) d -> p a t d", a=2)
        meanvar3 = [meanvar, meanvar2]
        stats3 = sb("stats3", [P, GT, 6])

        bank = [ps(f"bank{i}", [P, 512]) for i in range(4)]
        pscore = ps("pscore", [P, 4, 2, 2 * P])
        ps_ret, ps_a, ps_b, ps_c = bank

        s_cst, s_x0, s_w = sem("s_cst"), sem("s_tokw"), sem("s_weights")
        s_x = [sem(f"s_xchunk{i}") for i in range(RING)]
        s_score = sem("s_score")
        s_top = sem("s_top")
        s_spread = sem("s_spread")
        s_idxps = sem("s_idxps")
        s_index = sem("s_index")
        s_gather = [sem(f"s_gather{g}") for g in range(G)]
        s_prep = sem("s_prep")
        s_b1t, s_b1 = sem("s_b1t"), sem("s_b1")
        s_scoreA, s_prod, s_zero = sem("s_scoreA"), sem("s_prod"), sem("s_zero")
        s_stat1, s_rs1, s_nm1, s_ln = sem("s_stat1"), sem("s_rs1"), sem("s_nm1"), sem("s_ln")
        s_t1, s_lnT, s_q, s_k, s_v, s_g = (sem(n) for n in ("s_t1", "s_lnT", "s_q", "s_k", "s_v", "s_g"))
        s_qc, s_kc, s_vc, s_gc = (sem(n) for n in ("s_qc", "s_kc", "s_vc", "s_gc"))
        s_sc, s_prob, s_ret, s_retc, s_tret = (sem(n) for n in ("s_sc", "s_prob", "s_ret", "s_retc", "s_tret"))
        s_sq, s_gvar = sem("s_sq"), sem("s_gvar")
        s_norm, s_normw, s_pre = sem("s_norm"), sem("s_normw"), sem("s_pre")
        s_th, s_act, s_tz, s_zT, s_wo = (sem(n) for n in ("s_th", "s_act", "s_tz", "s_zT", "s_wo"))
        s_stat2, s_rs2, s_nm2, s_xhat, s_hn2 = (sem(n) for n in ("s_stat2", "s_rs2", "s_nm2", "s_xhat", "s_hn2"))
        s_t3, s_xnT, s_r, s_logit, s_tc = (sem(n) for n in ("s_t3", "s_xnT", "s_r", "s_logit", "s_tc"))
        s_rt = sem("s_router")
        s_e2, s_mixed = sem("s_e2"), sem("s_mixed")
        s_pick, s_rank, s_rankc, s_pos, s_row = (sem(n) for n in ("s_pick", "s_rank", "s_rankc", "s_pos", "s_row"))
        s_scat, s_zrow, s_pad, s_ztile = sem("s_scattered"), sem("s_zero_rows"), sem("s_padded"), sem("s_zero_tile")
        s_cnt, s_slot, s_tab, s_tabT = sem("s_counts"), sem("s_slot"), sem("s_table"), sem("s_tableT")
        s_xin = [sem(f"s_xin{u}") for u in range(4)]
        s_pairs = [sem(f"s_pairs{u}") for u in range(4)]
        s_ids, s_dest = sem("s_ids"), sem("s_dest")
        s_xt, s_xTc, s_w1, s_up, s_hid, s_down, s_y = (sem(n) for n in ("s_xt", "s_xTc", "s_w1", "s_up", "s_hid", "s_down", "s_y"))
        s_load = [sem("s_load0"), sem("s_load1")]
        s_weigh1, s_weigh2, s_both, s_stat3, s_rs4, s_nm4, s_norm4, s_mul4, s_fin = (sem(n) for n in (
            "s_weigh1", "s_weigh2", "s_both", "s_stat3", "s_rs4", "s_nm4", "s_norm4", "s_mul4", "s_fin"))
        s_hb = sem("s_hb")
        s_out = [sem("s_out0"), sem("s_out1")]

        s_half, s_w0, s_bias, s_parts = sem("s_half"), sem("s_w0"), sem("s_bias"), sem("s_parts")
        s_wbig = sem("s_wbig")
        down = [pscore[:, i].rearrange("p a b -> p (a b)") for i in range(2)]

        block = ctx.enter_context(nc.Block())

        def chunks_of(half, owner):
            return [half * NCH + k for k in range(NCH) if (half == 0 and (k % 3 == 2 or k == 0)) == bool(owner)]

        def here(p):
            return not isinstance(p, int) or 0 <= p < G

        def last_group(p):
            return isinstance(p, int) and p == G - 1

        def mix_schedule(eng, step):
            for i in range(-2, 3):
                step(i)
            with eng.Fori(3, G - 2) as i:
                step(i)
            for i in range(G - 2, G + 3):
                step(i)

        def repeat(eng, step, count, unroll):
            last = (count - 1) // unroll
            for u in range(unroll):
                step(0, u)
            with eng.Fori(1, last) as i:
                for u in range(unroll):
                    step(i, u)
            for u in range(count - last * unroll):
                step(last, u)

        def exists(n, count):
            return not isinstance(n, int) or 0 <= n < count

        def ahead(i, u, by, unroll):
            i, u = i + (u + by) // unroll, (u + by) % unroll
            return i * unroll + u, i, u

        def used_up(eng, c):
            for owner, s_used in enumerate((s_score, s_scoreA)):
                mine = [n for h in range(HALVES) for n in chunks_of(h, owner)]
                if c in mine:
                    eng.wait_ge(s_used, mine.index(c) + 1)

        def scored(eng, half):
            for owner, s_used in enumerate((s_score, s_scoreA)):
                eng.wait_ge(s_used, sum(len(chunks_of(h, owner)) for h in range(half + 1)))

        @block.sync
        def _(sp):
            sp.dma_start(tokw[:, :], tok_w[0].partition_broadcast(P)).then_inc(s_x0, 16)
            sp.dma_start(tokb[:, :], tok_b.partition_broadcast(P)).then_inc(s_x0, 16)
            for c in range(HALVES * NCH):
                half, k = c // NCH, c % NCH
                if c >= RING:
                    used_up(sp, c - RING)
                sp.dma_start(xring[:, c % RING, :], x_chunks[half * P:(half + 1) * P, k, :]).then_inc(s_x[c % RING], 16)
                if c == 2:
                    sp.dma_start(cst[:, :], consts).then_inc(s_cst, 16)
            for e in range(E):
                sp.dma_start(w1_s[:, e, 0:HID], w1[e]).then_inc(s_wbig, 16)
                sp.dma_start(w2_s[:, e, :, :], w2[e].rearrange("(c p) d -> p c d", p=P)).then_inc(s_wbig, 16)
            sp.wait_ge(s_zrow, 2)
            sp.dma_start(routed[E * REGION:E * REGION + P, :], zrow[:, :]).then_inc(s_ztile, 16)
            sp.wait_ge(s_cnt, 2)
            for e in range(E):
                end = sp.value_load(rowend[0:1, e:e + 1], min_val=0, max_val=E * REGION - P)
                sp.dma_start(routed[ds(end, P), :], zrow[:, :]).then_inc(s_pad, 16)
            sp.wait_ge(s_tabT, 1)
            sp.wait_ge(s_scat, 16 * 2 * TILES)
            sp.wait_ge(s_pad, 16 * E)
            sp.wait_ge(s_ztile, 16)

            def load_slot(i, u):
                s = i * 4 + u
                row = sp.value_load(table[0:1, ds(s, 1)], min_val=0, max_val=E * REGION)
                if exists(s - 4, SLOTS):
                    sp.wait_ge(s_xt, s - 3)
                    sp.wait_ge(s_ids, s - 3)
                sp.dma_start(xin[:, u, :], routed[ds(row, P), :]).then_inc(s_xin[u], 16)

            repeat(sp, load_slot, SLOTS, 4)
            for u in range(4):
                sp.wait_ge(s_pairs[u], 16 * len(range(u, SLOTS, 4)))
            for g in range(G):
                if g >= 2:
                    sp.wait_ge(s_load[g % 2], 16 * (g // 2))
                sp.dma_start(ypair[:, g, :, :, :], pair_groups[g]).then_inc(s_load[g % 2], 16)

            def store(i, odd):
                g = i * 2 + odd
                sp.wait_ge(s_fin, g + 1)
                sp.dma_start(out_groups[g], yo[:, odd, :, :]).then_inc(s_out[odd], 16)

            repeat(sp, store, G, 2)
            for odd in range(2):
                sp.wait_ge(s_out[odd], 16 * (G // 2) + 1)

        @block.gpsimd
        def _(pool):
            nc.gpsimd.memset(vpad[:, :, :, :], 0.0).then_inc(s_zero, 1)
            nc.gpsimd.memset(halves[:, :], -0.5).then_inc(s_half, 1)
            pool.wait_ge(s_half, 1)

            def power(dst, base):
                return nc.gpsimd.tensor_tensor(dst, base, halves[:, 0:base.shape[1]], ALU.pow)

            def products(chunks):
                for c in chunks:
                    pool.wait_ge(s_x[c % RING], 16 * (c // RING + 1))
                    rows = xring[:, c % RING, :].rearrange("p (t d) -> p t d", d=D)
                    nc.gpsimd.tensor_tensor(rows, rows, tokw[:, :].unsqueeze(1).to_broadcast([P, CH, D]),
                                            ALU.mult).then_inc(s_prod, 1)

            def gather(g):
                for t in range(g * GT, (g + 1) * GT):
                    nc.gpsimd.indirect_dma_start(
                        out=hsel[:, t, :], out_offset=None, in_=x_tokens,
                        in_offset=bass.IndirectOffsetOnAxis(ap=index[:, t:t + 1], axis=0)).then_inc(s_gather[g], 16)

            def scatter(choice):
                for t in range(GT):
                    n = choice * GT + t
                    nc.gpsimd.indirect_dma_start(
                        out=routed, out_offset=bass.IndirectOffsetOnAxis(ap=pos[:, n:n + 1], axis=0),
                        in_=xrow[:, choice, t, :], in_offset=None).then_inc(s_scat, 16)

            def step(i):
                if isinstance(i, int) and i == 2:
                    pool.wait_ge(s_index, 2)
                    for g in range(G // 2, G):
                        gather(g)
                if here(i - 2):
                    pool.wait_ge(s_stat2, i - 1)
                    if here(i - 3):
                        pool.wait_ge(s_hn2, (i - 2) * GT)
                    power(rstd23[:, :, :].rearrange("p a b -> p (a b)"),
                          var23[:, :, :].rearrange("p a b -> p (a b)")).then_inc(s_rs2, 1)
                    pool.wait_ge(s_rs2, i - 1)
                    nc.gpsimd.tensor_tensor(nm23[:, :, :], rstd23[:, :, :], minus2[:, :].unsqueeze(1).to_broadcast([P, 2, GT]),
                                            ALU.mult).then_inc(s_nm2, 1)
                if here(i - 1):
                    if here(i - 2):
                        pool.wait_ge(s_pre, i - 1)
                    pool.wait_ge(s_norm, i)
                    if here(i - 3):
                        pool.wait_ge(s_pos, (i - 2) * 2)
                        pool.wait_ge(s_row, i - 2)
                    nc.gpsimd.tensor_tensor(normw[:, :, :], normed[:, :, :],
                                            gnw[:, :].unsqueeze(1).to_broadcast([P, GT, D]), ALU.mult).then_inc(s_normw, 1)
                    pool.wait_ge(s_normw, i)
                    pool.wait_ge(s_gc, i)
                    nc.gpsimd.tensor_tensor(pre[:, :, :], normw[:, :, :], hn2[:, ds((i - 1) * GT, GT), :], ALU.add).then_inc(s_pre, 1)
                if here(i + 2):
                    pool.wait_ge(s_stat1, i + 3)
                    power(rstd1[:, :], var1[:, :]).then_inc(s_rs1, 1)
                if isinstance(i, int) and i <= 0:
                    gather(i + 3)
                if here(i - 3):
                    if not here(i - 1):
                        pool.wait_ge(s_pos, (i - 2) * 2)
                        pool.wait_ge(s_row, i - 2)
                    scatter(0)
                    scatter(1)

            pool.wait_ge(s_x0, 32)
            products(chunks_of(0, 1))
            pool.wait_ge(s_index, 1)
            gather(0)
            mix_schedule(pool, step)
            def place(n, u):
                pool.wait_ge(s_ids, n + 1)
                nc.gpsimd.tensor_tensor(dest[:, u:u + 1], ids[:, u, 0:1], ids[:, u, 1:2], ALU.add).then_inc(s_dest, 1)

            def scatter_slot(i, u):
                s = i * 4 + u
                pool.wait_ge(s_dest, s + 1)
                pool.wait_ge(s_y, s + 1)
                n, _, v = ahead(i, u, 1, 4)
                if exists(n, SLOTS):
                    place(n, v)
                nc.gpsimd.indirect_dma_start(
                    out=pairs, out_offset=bass.IndirectOffsetOnAxis(ap=dest[:, u:u + 1], axis=0),
                    in_=yslot[:, u, :], in_offset=None,
                    bounds_check=PAIRS - 1, oob_is_err=False).then_inc(s_pairs[u], 16)

            place(0, 0)
            repeat(pool, scatter_slot, SLOTS, 4)

            def weigh(n, i, odd):
                pool.wait_ge(s_load[odd], (i + 1) * 16)
                if exists(n - 2, G):
                    pool.wait_ge(s_both, n - 1)
                nc.gpsimd.tensor_tensor(weighed2[odd][:, :, :], ypair[:, ds(n, 1), :, 1, :].rearrange("p a t d -> p (a t) d"),
                                        conf12[:, ds(n * GT, GT), 1:2].to_broadcast([P, GT, D]), ALU.mult).then_inc(s_weigh2, 1)

            def finish(i, odd):
                g = i * 2 + odd
                n, ni, v = ahead(i, odd, 2, 2)
                pool.wait_ge(s_stat3, g + 1)
                power(rstd4[:, odd, :], var4[:, odd, :]).then_inc(s_rs4, 1)
                if exists(n, G):
                    weigh(n, ni, v)
                pool.wait_ge(s_norm4, g + 1)
                if exists(g - 2, G):
                    pool.wait_ge(s_fin, g - 1)
                nc.gpsimd.tensor_tensor(yw[odd][:, :, :], y[odd][:, :, :], outg[:, :].unsqueeze(1).to_broadcast([P, GT, D]),
                                        ALU.mult).then_inc(s_mul4, 1)

            pool.wait_ge(s_rt, 4)
            weigh(0, 0, 0)
            weigh(1, 0, 1)
            repeat(pool, finish, G, 2)

        @block.scalar
        def _(act):
            small = [(wq_s[:, :], wq), (wk_s[:, :], wk), (wo_s[:, :], wo), (wvg[:, 0, :], wv), (wvg[:, 1, :], wg), (wgate[:, :], ffn_wg),
                     (gnw[:, :], gn_w.partition_broadcast(P)), 
                     (outg[:, :], out_g.partition_broadcast(P)), (outb[:, :], out_b.partition_broadcast(P)),
                     (lng[:, :], ln_g.unsqueeze(1)), (lnb[:, :], ln_b.unsqueeze(1)),
                     (b1_rows[:, :], b1.rearrange("e (c p) -> (e c) p", p=P)), (bias[0:E, :], b2), (bias[E:E + 1, :], gn_b.unsqueeze(0))]
            assert len(small) == SMALL

            def load_weights():
                for dst, src in small:
                    act.dma_start(dst, src).then_inc(s_w, 16)

            def hsel_g(g, j):
                return hsel[:, ds(g * GT + j, 1), :].rearrange("p a d -> p (a d)")

            def sums(chunks):
                for c in chunks:
                    half = c // NCH
                    act.wait_ge(s_prod, [n for h in range(HALVES) for n in chunks_of(h, 1)].index(c) + 1)
                    for t in range(CH):
                        row = xring[:, c % RING, t * D:(t + 1) * D]
                        n = c % NCH * CH + t
                        last = nc.scalar.activation(row, row, ACT.Copy, accum_out=score[:, half, n:n + 1])
                    last.then_inc(s_scoreA, 1)

            def step(i):
                if here(i - 3):
                    act.wait_ge(s_t3, i - 2)
                    if here(i - 4):
                        act.wait_ge(s_r, i - 3)
                    nc.scalar.activation(xnTg[:, :], ps_b[:, :], ACT.Identity,
                                         scale=lng[:, 0:1], bias=lnb[:, 0:1]).then_inc(s_xnT, 1)
                if here(i - 1):
                    act.wait_ge(s_ret, i)
                    nc.scalar.activation(retT[:, :, :].rearrange("p a b -> p (a b)"), ps_ret[:, :], ACT.Copy).then_inc(s_retc, 1)
                if here(i - 2):
                    act.wait_ge(s_pre, i - 1)
                    nc.scalar.activation(th[:, :, :], pre[:, :, :], ACT.Tanh, scale=0.5).then_inc(s_th, 1)
                if here(i + 1):
                    act.wait_ge(s_nm1, i + 2)
                    if here(i):
                        act.wait_ge(s_t1, i + 1)
                    for j in range(GT):
                        last = nc.scalar.activation(ln[:, j, :], hsel_g(i + 1, j), ACT.Identity,
                                                    scale=rstd1[:, j:j + 1], bias=nm1[:, j:j + 1])
                    last.then_inc(s_ln, 1)
                if here(i):
                    act.wait_ge(s_v, i + 1)
                    act.wait_ge(s_g, i + 1)
                    heads = ps_a[:, :].rearrange("p (t h e d) -> p t h e d", t=GT, e=2, d=DH)
                    if isinstance(i, int) and i == 0:
                        act.wait_ge(s_zero, 1)
                    for odd in range(2):
                        nc.scalar.activation(vpad[:, :, odd, :].rearrange("p t (h e d) -> p t h e d", e=2, d=DH)[:, :, :, odd, :],
                                             heads[:, :, :, odd, :], ACT.Copy).then_inc(s_vc, 1)
                    nc.scalar.activation(hn2[:, ds(i * GT, GT), :].rearrange("p a b -> p (a b)"), ps_b[:, :], ACT.Copy).then_inc(s_gc, 1)
                if here(i - 2):
                    act.wait_ge(s_tz, i - 1)
                    nc.scalar.activation(actT[:, :], ps_c[:, :], ACT.Copy).then_inc(s_zT, 1)
                if here(i - 1):
                    act.wait_ge(s_tret, i)
                    if here(i - 2):
                        act.wait_ge(s_gvar, i - 1)
                    nc.scalar.activation(square[:, :], ps_a[:, :], ACT.Square).then_inc(s_sq, 1)
                if here(i + 1):
                    act.wait_ge(s_t1, i + 2)
                    nc.scalar.activation(lnT[:, :], ps_b[:, :], ACT.Copy).then_inc(s_lnT, 1)
                if here(i + 1):
                    act.wait_ge(s_k, i + 2)
                    nc.scalar.activation(kT[:, :], ps_b[:, :], ACT.Copy).then_inc(s_kc, 1)
                if here(i + 1):
                    act.wait_ge(s_q, i + 2)
                    for odd in range(2):
                        nc.scalar.activation(qeo[:, :, odd, :], ps_c[:, :].rearrange("p (t n) -> p t n", t=GT), ACT.Copy,
                                             scale=cst[:, C_PAR + odd:C_PAR + odd + 1]).then_inc(s_qc, 1)
                if here(i - 3):
                    if here(i - 4):
                        act.wait_ge(s_scat, (i - 3) * 2 * GT * 16)
                    nc.scalar.activation(xrow[:, :, :, 0:D], xhat[:, :, :].unsqueeze(1).to_broadcast([P, 2, GT, D]),
                                         ACT.Copy).then_inc(s_row, 1)
                if here(i - 2):
                    act.wait_ge(s_nm2, i - 1)
                    if here(i - 3):
                        act.wait_ge(s_t3, i - 2)
                        act.wait_ge(s_row, i - 2)
                    for j in range(GT):
                        last = nc.scalar.activation(xhat[:, j, :], hsel_g(i - 2, j), ACT.Identity,
                                                    scale=rstd3[:, j:j + 1], bias=nm3[:, j:j + 1])
                    last.then_inc(s_xhat, 1)
                if here(i - 2):
                    for j in range(GT):
                        nc.scalar.activation(hn2[:, ds((i - 2) * GT + j, 1), :].rearrange("p a d -> p (a d)"), hsel_g(i - 2, j),
                                             ACT.Identity, scale=rstd2[:, j:j + 1], bias=nm2[:, j:j + 1]).then_inc(s_hn2, 1)

            sums(chunks_of(0, 1)[:1])
            load_weights()
            sums(chunks_of(0, 1)[1:])
            act.wait_ge(s_cst, 16)
            act.wait_ge(s_w, 16 * SMALL)
            act.wait_ge(s_w0, 6)
            for n, part in enumerate((bias_hi, bias_mid, bias_lo)):
                act.dma_start(bias_rows[n], part[:, :]).then_inc(s_bias, 16)
            act.wait_ge(s_bias, 48)
            act.dma_start(bias_parts[:, :, :], bias_rows).then_inc(s_parts, 16)
            mix_schedule(act, step)
            act.wait_ge(s_rt, 1)
            nc.scalar.activation(e2[:, :], gap[:, :], ACT.Exp).then_inc(s_e2, 1)

            def xT_out(n, u):
                act.wait_ge(s_xt, n + 1)
                if exists(n - 2, SLOTS):
                    act.wait_ge(s_up, n - 1)
                nc.scalar.activation(xT[:, u % 2, :], bank[u % 2][:, 0:P], ACT.Identity,
                                     scale=lng[:, 0:1], bias=lnb[:, 0:1]).then_inc(s_xTc, 1)

            def hidden(n, u):
                act.wait_ge(s_up, n + 1)
                if exists(n - 2, SLOTS):
                    act.wait_ge(s_down, n - 1)
                for c in range(HC):
                    nc.scalar.activation(hid[:, u % 2, c, :], bank[2 + u % 2][:, c * P:(c + 1) * P], ACT.Gelu_apprx_tanh,
                                         bias=w1_now[:, u % 2, HID + c:HID + c + 1]).then_inc(s_hid, 1)

            def slot(i, u):
                n, _, v = ahead(i, u, 2, 4)
                if exists(n, SLOTS):
                    xT_out(n, v)
                n, _, v = ahead(i, u, 1, 4)
                if exists(n, SLOTS):
                    hidden(n, v)

            xT_out(0, 0)
            xT_out(1, 1)
            hidden(0, 0)
            repeat(act, slot, SLOTS, 4)

            def weigh(n, odd):
                for j in range(GT):
                    last = nc.scalar.activation(weighed1[odd][:, j, :], ypair[:, ds(n, 1), j, 0, :].rearrange("p a d -> p (a d)"),
                                                ACT.Copy, scale=conf12[:, ds(n * GT + j, 1), 0:1].rearrange("p a b -> p (a b)"))
                last.then_inc(s_weigh1, 1)

            def finish(i, odd):
                g = i * 2 + odd
                n, ni, v = ahead(i, odd, 2, 2)
                act.wait_ge(s_nm4, g + 1)
                if exists(g - 2, G):
                    act.wait_ge(s_mul4, g - 1)
                if exists(n, G):
                    act.wait_ge(s_load[v], (ni + 1) * 16)
                for j in range(GT):
                    last = nc.scalar.activation(y[odd][:, j, :], acc[odd][:, j, :], ACT.Identity,
                                                scale=rstd4[:, odd, j:j + 1], bias=nm4[:, odd, j:j + 1])
                last.then_inc(s_norm4, 1)
                if exists(n, G):
                    weigh(n, v)

            act.wait_ge(s_rt, 4)
            for g in range(2):
                act.wait_ge(s_load[g], 16)
                weigh(g, g)
            repeat(act, finish, G, 2)

        @block.vector
        def _(dve):
            def prepare():
                dve.wait_ge(s_w, 16 * SMALL)
                wv_heads = wvg[:, 0, :].rearrange("p (h d) -> p h d", h=HEADS)
                nc.vector.tensor_reduce(vmean[:, :], wv_heads, AX_X, ALU.add).then_inc(s_w0, 1)
                dve.wait_ge(s_w0, 1)
                nc.vector.scalar_tensor_tensor(out=wv_heads, in0=vmean[:, :].unsqueeze(2).to_broadcast([P, HEADS, DH]),
                                               scalar=-1.0 / DH, in1=wv_heads, op0=ALU.mult, op1=ALU.add).then_inc(s_prep, 1)
                nc.vector.tensor_scalar(wo_s[:, :], wo_s[:, :], 0.5, None, ALU.mult).then_inc(s_prep, 1)
                nc.vector.tensor_copy(bias_hi[:, :], bias[:, :]).then_inc(s_w0, 1)
                dve.wait_ge(s_w0, 2)
                nc.vector.tensor_tensor(bias_rest[:, :], bias[:, :], bias_hi[:, :], ALU.subtract).then_inc(s_w0, 1)
                dve.wait_ge(s_w0, 3)
                nc.vector.tensor_copy(bias_mid[:, :], bias_rest[:, :]).then_inc(s_w0, 1)
                dve.wait_ge(s_w0, 4)
                nc.vector.tensor_tensor(bias_rest2[:, :], bias_rest[:, :], bias_mid[:, :], ALU.subtract).then_inc(s_w0, 1)
                dve.wait_ge(s_w0, 5)
                nc.vector.tensor_copy(bias_lo[:, :], bias_rest2[:, :]).then_inc(s_w0, 1)
                nc.vector.memset(ones3[:, :], 1.0).then_inc(s_prep, 1)
                dve.wait_ge(s_b1t, 1)
                nc.vector.tensor_copy(w1_s[:, :, HID:HID + HC], ps_a[:, 0:E * HC].rearrange("p (e c) -> p e c", c=HC)).then_inc(s_b1, 1)
                nc.vector.memset(ones[:, :], 1.0)
                nc.vector.memset(before[:, :], 0.0)
                nc.vector.memset(zrow[:, 0:D], 0.0).then_inc(s_zrow, 1)
                nc.vector.memset(zrow[:, D:XW], float(PAIRS)).then_inc(s_zrow, 1)
                for choice in range(2):
                    nc.vector.memset(xrow[:, choice, :, D + 1], float(choice))
                nc.vector.tensor_copy(earlier[:, :], cst[:, C_EARLIER:C_EARLIER + P]).then_inc(s_prep, 1)
                nc.vector.tensor_scalar(xrow[:, :, :, D], cst[:, C_TOKEN:C_TOKEN + GT].unsqueeze(1).to_broadcast([P, 2, GT]),
                                        -2.0 * GN, None, ALU.add)

            dve.wait_ge(s_x0, 32)
            steps = 0

            def chain(instruction):
                nonlocal steps
                steps += 1
                instruction.then_inc(s_top, 1)
                dve.wait_ge(s_top, steps)

            def scores(chunks):
                for c in chunks:
                    half = c // NCH
                    dve.wait_ge(s_x[c % RING], 16 * (c // RING + 1))
                    for t in range(CH):
                        n = c % NCH * CH + t
                        row = xring[:, c % RING, t * D:(t + 1) * D]
                        last = nc.vector.tensor_tensor_reduce(
                            out=row, in0=row, in1=tokw[:, :],
                            scale=1.0, scalar=0.0, op0=ALU.mult, op1=ALU.add, accum_out=score[:, half, n:n + 1])
                    last.then_inc(s_score, 1)

            def select(half):
                scored(dve, half)
                dve.wait_ge(s_cst, 16)
                sc = score[:, half, :]
                chain(nc.vector.tensor_scalar(sc, sc, tokb[:, 0:1], None, ALU.add))
                chain(nc.vector.max(best[:, 0:8], sc))
                chain(nc.vector.max_index(besti[:, 0:8], best[:, 0:8], sc))
                chain(nc.vector.match_replace(score2[:, :], best[:, 0:8], sc, LOWEST))
                chain(nc.vector.max(best[:, 8:16], score2[:, :]))
                chain(nc.vector.max_index(besti[:, 8:16], best[:, 8:16], score2[:, :]))
                chain(nc.vector.tensor_scalar(bestf[:, :], besti[:, :], cst[:, C_BASE:C_BASE + 1], float(half * P * BLOCK),
                                              ALU.add, ALU.add))
                nc.vector.tensor_tensor(spread[:, :, :], bestf[:, :].unsqueeze(1).to_broadcast([P, 8, TOPK]),
                                        cst[:, C_ROW8:C_ROW8 + 8].unsqueeze(2).to_broadcast([P, 8, TOPK]),
                                        ALU.mult).then_inc(s_spread, 1)
                dve.wait_ge(s_idxps, half + 1)
                nc.vector.tensor_copy(index[:, half * 16:half * 16 + 16], ps_c[:, 0:16]).then_inc(s_index, 1)

            def statistics(stats_, meanvar_, rows):
                for j in range(GT):
                    nc.vector.bn_stats(stats_[:, j, :], rows[j])
                dve.drain()
                for j in range(GT):
                    nc.vector.bn_aggr(meanvar_[:, j, :], stats_[:, j, :])
                dve.drain()

            def hsel_g(g, j):
                return hsel[:, ds(g * GT + j, 1), :].rearrange("p a d -> p (a d)")

            def minus_mean(dst, meanvar_, rstd):
                return nc.vector.scalar_tensor_tensor(out=dst, in0=meanvar_[:, :, 0], scalar=-1.0, in1=rstd,
                                                      op0=ALU.mult, op1=ALU.mult)

            def inverse_root(y, v):
                a, b = root_a[:, :], root_b[:, :]
                nc.vector.tensor_scalar(a.bitcast(I32), v.bitcast(I32), 1, None, ALU.logical_shift_right)
                nc.vector.tensor_scalar(b, v, -0.5, None, ALU.mult)
                dve.drain()
                nc.vector.tensor_scalar(y.bitcast(I32), a.bitcast(I32), -1.0, float(0x5F3759DF), ALU.mult, ALU.add)
                for _ in range(3):
                    dve.drain()
                    nc.vector.tensor_tensor(a, y, y, ALU.mult)
                    dve.drain()
                    nc.vector.tensor_tensor(a, a, b, ALU.mult)
                    dve.drain()
                    nc.vector.scalar_tensor_tensor(out=y, in0=a, scalar=1.5, in1=y, op0=ALU.add, op1=ALU.mult)
                dve.drain()

            def probs(g, r):
                dve.wait_ge(s_sc, g * 2 + r + 1)
                for t in (2 * r, 2 * r + 1):
                    nc.vector.tensor_tensor(prob[:, t, :, :].rearrange("p (j i) n -> p j (i n)", i=2), pscore[:, :, t % 2, :],
                                            decay, ALU.mult).then_inc(s_prob, 1)

            def head_variances(i):
                dve.wait_ge(s_sq, i)
                nc.vector.tensor_reduce(gvar[:, :], square[:, :].rearrange("p (a d) -> p a d", d=DH), AX_X, ALU.add)
                dve.drain()
                nc.vector.tensor_scalar(gvar2[:, :], gvar[:, :], 1.0 / DH, EPS, ALU.mult, ALU.add).then_inc(s_gvar, 1)

            def norm_heads():
                inverse_root(grstd[:, :], gvar2[:, :])
                nc.vector.tensor_tensor(normed[:, :, :].rearrange("p t (h d) -> p (t h) d", d=DH),
                                        ps_a[:, :].rearrange("p (a d) -> p a d", d=DH),
                                        grstd[:, :].unsqueeze(2).to_broadcast([P, GT * HEADS, DH]), ALU.mult).then_inc(s_norm, 1)

            def step(i):
                if here(i):
                    probs(i, 0)
                if here(i - 2):
                    dve.wait_ge(s_th, i - 1)
                    nc.vector.scalar_tensor_tensor(out=act_s[:, :, :], in0=th[:, :, :], scalar=1.0, in1=pre[:, :, :],
                                                   op0=ALU.add, op1=ALU.mult).then_inc(s_act, 1)
                if here(i + 1):
                    dve.wait_ge(s_rs1, i + 2)
                    minus_mean(nm1[:, :], meanvar, rstd1[:, :]).then_inc(s_nm1, 1)
                if here(i - 3):
                    dve.wait_ge(s_r, i - 2)
                    nc.vector.tensor_copy(logit[:, :, :], ps_ret[:, 0:GT * E].rearrange("p (t e) -> p t e", e=E)).then_inc(s_logit, 1)
                    dve.drain()
                    for j in range(GT):
                        nc.vector.max(topg[:, j, :], logit[:, j, :])
                    dve.drain()
                    for j in range(GT):
                        nc.vector.max_index(topig[:, j, :], topg[:, j, :], logit[:, j, :])
                    nc.vector.tensor_copy(top12[:, ds((i - 3) * GT, GT), :], topg[:, :, 0:2]).then_inc(s_tc, 1)
                    dve.drain()
                    nc.vector.tensor_copy(topf[:, :, :], topig[:, :, 0:2].rearrange("p t k -> p k t"))
                    dve.drain()
                    nc.vector.tensor_tensor(pick[:, :, :, :].rearrange("p k t e -> p (k t) e"),
                                            cst[:, C_IOTA:C_IOTA + E].unsqueeze(1).to_broadcast([P, 2 * GT, E]),
                                            topf[:, :, :].rearrange("p k t -> p (k t)").unsqueeze(2).to_broadcast([P, 2 * GT, E]),
                                            ALU.is_equal)
                    dve.drain()
                    nc.vector.tensor_tensor(chosen[:, :, :], pick[:, 0], pick[:, 1], ALU.add).then_inc(s_pick, 1)
                    dve.drain()
                    nc.vector.tensor_reduce(chosen_sum[:, :], chosen[:, :, :].rearrange("p t e -> p e t"), AX_X, ALU.add)
                if isinstance(i, int) and i in (0, 1):
                    scores(chunks_of(1, 0)[6:7] if i == 0 else chunks_of(1, 0)[7:])
                    if i == 1:
                        select(1)
                if last_group(i - 1):
                    head_variances(i)
                    dve.drain()
                    norm_heads()
                if here(i - 2):
                    dve.wait_ge(s_wo, i - 1)
                    tiles = hsel[:, ds((i - 2) * GT, GT), :]
                    nc.vector.tensor_tensor(tiles, ps_c[:, :].rearrange("p (t d) -> p t d", t=GT), tiles, ALU.add).then_inc(s_mixed, 1)
                    dve.drain()
                    statistics(stats[:, 1], meanvar2, [hsel_g(i - 2, j) for j in range(GT)])
                    if here(i - 3):
                        dve.wait_ge(s_nm2, i - 2)
                    nc.vector.tensor_scalar(minus2[:, :], meanvar2[:, :, 0], -1.0, None, ALU.mult)
                    nc.vector.tensor_scalar(var2, meanvar2[:, :, 1], EPS, None, ALU.add)
                    nc.vector.tensor_scalar(var3, meanvar2[:, :, 1], 1.0 + EPS, EPS * EPS, ALU.mult, ALU.add)
                    dve.drain().then_inc(s_stat2, 1)
                if here(i - 3):
                    dve.wait_ge(s_rank, i - 2)
                    nc.vector.tensor_tensor(rank[:, :, :], ps_ret[:, 0:GT * E].rearrange("p (t e) -> p t e", e=E),
                                            cst[:, C_REGION:C_REGION + E].unsqueeze(1).to_broadcast([P, GT, E]),
                                            ALU.add).then_inc(s_rankc, 1)
                if here(i - 1) and not last_group(i - 1):
                    head_variances(i)
                if here(i):
                    probs(i, 1)
                if here(i - 3):
                    dve.drain()
                    nc.vector.tensor_tensor(before[:, :], before[:, :], chosen_sum[:, :], ALU.add).then_inc(s_rankc, 1)
                    nc.vector.tensor_tensor(rank_pick[:, :, :, :], pick[:, :, :, :],
                                            rank[:, :, :].unsqueeze(1).to_broadcast([P, 2, GT, E]), ALU.mult)
                    dve.drain()
                    nc.vector.tensor_reduce(posf[:, :, :], rank_pick[:, :, :, :], AX_X, ALU.add)
                    dve.drain()
                    if here(i - 4):
                        dve.wait_ge(s_scat, (i - 3) * 2 * GT * 16)
                    nc.vector.tensor_scalar(xrow[:, :, :, D], xrow[:, :, :, D], 2.0 * GN, None, ALU.add).then_inc(s_pos, 1)
                    nc.vector.tensor_copy(pos[:, :], posf[:, :, :].rearrange("p k t -> p (k t)")).then_inc(s_pos, 1)
                if here(i - 1) and not last_group(i - 1):
                    dve.drain()
                    norm_heads()
                if here(i + 2):
                    if isinstance(i, int):
                        dve.wait_ge(s_gather[i + 2], 16 * GT)
                    else:
                        dve.wait_ge(s_gather[G - 1], 16 * GT)
                    statistics(stats[:, 0], meanvar, [hsel_g(i + 2, j) for j in range(GT)])
                    if here(i + 1):
                        dve.wait_ge(s_ln, i + 2)
                    nc.vector.tensor_scalar(var1[:, :], meanvar[:, :, 1], EPS, None, ALU.add).then_inc(s_stat1, 1)
                if isinstance(i, int) and i < 0:
                    scores(chunks_of(1, 0)[1:3] if i == -2 else chunks_of(1, 0)[3:6])

            scores(chunks_of(0, 0))
            select(0)
            prepare()
            scores(chunks_of(1, 0)[0:1])
            mix_schedule(dve, step)

            done = 0

            def seq(instruction):
                nonlocal done
                done += 1
                instruction.then_inc(s_slot, 1)
                dve.wait_ge(s_slot, done)

            dve.wait_ge(s_cnt, 1)
            seq(nc.vector.tensor_copy(count[:, :], ps_b[:, 0:E]))
            nc.vector.tensor_tensor(rowend[:, :], count[:, :], cst[:, C_REGION:C_REGION + E], ALU.add).then_inc(s_cnt, 1)
            seq(nc.vector.tensor_tensor(reached[:, :, :], count[:, :].unsqueeze(2).to_broadcast([P, E, TILES]),
                                        cst[:, C_TILE:C_TILE + TILES].unsqueeze(1).to_broadcast([P, E, TILES]), ALU.is_gt))
            seq(nc.vector.tensor_reduce(ntiles[:, :], reached[:, :, :], AX_X, ALU.add))
            seq(nc.vector.tensor_tensor(tri[:, :, :], ntiles[:, :].unsqueeze(1).to_broadcast([P, E, E]),
                                        cst[:, C_TRI8:C_TRI8 + E * E].rearrange("p (a b) -> p a b", b=E), ALU.mult))
            seq(nc.vector.tensor_reduce(ends[:, :], tri[:, :, :], AX_X, ALU.add))
            seq(nc.vector.tensor_scalar(passed[:, :], ends[:, :], cst[:, C_SLOT:C_SLOT + 1], None, ALU.is_le))
            seq(nc.vector.tensor_scalar(jump[:, :], ntiles[:, :], -float(P), float(REGION), ALU.mult, ALU.add))
            seq(nc.vector.tensor_tensor(jumps[:, :], jump[:, :], passed[:, :], ALU.mult))
            seq(nc.vector.tensor_reduce(slot_row[:, :], jumps[:, 0:E - 1], AX_X, ALU.add))
            seq(nc.vector.tensor_reduce(slot_e[:, :], passed[:, 0:E - 1], AX_X, ALU.add))
            seq(nc.vector.tensor_scalar(slot_row[:, :], slot_row[:, :], cst[:, C_BASE:C_BASE + 1], -float(E * REGION),
                                        ALU.add, ALU.add))
            seq(nc.vector.tensor_scalar(slot_in[:, :], passed[:, E - 1:E], -1.0, 1.0, ALU.mult, ALU.add))
            seq(nc.vector.tensor_tensor(slot_row[:, :], slot_row[:, :], slot_in[:, :], ALU.mult))
            nc.vector.tensor_scalar(slot_cols[:, 0:1], slot_row[:, :], float(E * REGION), None, ALU.add).then_inc(s_tab, 1)
            nc.vector.tensor_copy(slot_cols[:, 1:2], slot_e[:, :]).then_inc(s_tab, 1)
            dve.wait_ge(s_tab, 3)
            nc.vector.tensor_copy(table[:, :], ps_c[0:1, 0:2 * P]).then_inc(s_tabT, 1)

            dve.wait_ge(s_tc, G)
            nc.vector.tensor_tensor(gap[:, :], top12[:, :, 1], top12[:, :, 0], ALU.subtract).then_inc(s_rt, 1)
            dve.wait_ge(s_e2, 1)
            nc.vector.tensor_scalar(esum[:, :], e2[:, :], 1.0, None, ALU.add).then_inc(s_rt, 1)
            dve.wait_ge(s_rt, 2)
            nc.vector.reciprocal(conf12[:, :, 0], esum[:, :]).then_inc(s_rt, 1)
            dve.wait_ge(s_rt, 3)
            nc.vector.tensor_tensor(conf12[:, :, 1], conf12[:, :, 0], e2[:, :], ALU.mult).then_inc(s_rt, 1)
            dve.wait_ge(s_rt, 4)
            dve.wait_ge(s_hn2, TILES)
            for g in range(G):
                tiles = hsel[:, g * GT:(g + 1) * GT, :]
                nc.vector.tensor_tensor(tiles, tiles, outb[:, :].unsqueeze(1).to_broadcast([P, GT, D]),
                                        ALU.add).then_inc(s_hb, 1)
            dve.wait_ge(s_hb, G)

            def first_weights(n, u):
                e = dve.value_load(table[0:1, ds(n + P, 1)], min_val=0, max_val=E - 1)
                nc.vector.tensor_copy(w1_now[:, u % 2, :], w1_s[:, ds(e, 1), :].rearrange("p a b -> p (a b)")).then_inc(s_w1, 1)

            def slot(i, u):
                s = i * 4 + u
                if exists(s - 4, SLOTS):
                    dve.wait_ge(s_pairs[u], i * 16)
                n, _, v = ahead(i, u, 2, 4)
                if exists(n, SLOTS):
                    dve.wait_ge(s_hid, (s + 1) * HC)
                dve.wait_ge(s_xin[u], (i + 1) * 16)
                nc.vector.tensor_copy(ids[:, u, :], xin[:, u, D:XW]).then_inc(s_ids, 1)
                if exists(n, SLOTS):
                    first_weights(n, v)
                dve.wait_ge(s_down, s + 1)
                nc.vector.tensor_copy(yslot[:, u, :], down[u % 2][:, 0:D]).then_inc(s_y, 1)

            dve.wait_ge(s_wbig, 16 * 2 * E)
            first_weights(0, 0)
            first_weights(1, 1)
            repeat(dve, slot, SLOTS, 4)

            def sum_up(n, i, odd):
                dve.wait_ge(s_weigh1, n + 1)
                dve.wait_ge(s_weigh2, n + 1)
                if exists(n - 2, G):
                    dve.wait_ge(s_norm4, n - 1)
                nc.vector.tensor_tensor(both[odd][:, :, :], weighed1[odd][:, :, :], weighed2[odd][:, :, :], ALU.add).then_inc(s_both, 1)
                dve.drain()
                nc.vector.tensor_tensor(acc[odd][:, :, :], both[odd][:, :, :], hn2[:, ds(n * GT, GT), :], ALU.add)
                dve.drain()

            def spread_of(n, odd):
                statistics(stats3, meanvar3[odd], [acc[odd][:, j, :] for j in range(GT)])
                nc.vector.tensor_scalar(var4[:, odd, :], meanvar3[odd][:, :, 1], EPS, None, ALU.add).then_inc(s_stat3, 1)

            def last_sum(n, i, odd):
                dve.wait_ge(s_mul4, n + 1)
                dve.wait_ge(s_out[odd], i * 16 + 1)
                nc.vector.tensor_tensor(yo[:, odd, :, :], yw[odd][:, :, :], hsel[:, ds(n * GT, GT), :],
                                        ALU.add).then_inc(s_fin, 1)

            def finish(i, odd):
                g = i * 2 + odd
                n, ni, v = ahead(i, odd, -1, 2)
                if exists(n, G):
                    last_sum(n, ni, v)
                dve.wait_ge(s_rs4, g + 1)
                minus_mean(nm4[:, odd, :], meanvar3[odd], rstd4[:, odd, :]).then_inc(s_nm4, 1)
                n, ni, v = ahead(i, odd, 1, 2)
                if exists(n, G):
                    sum_up(n, ni, v)
                    spread_of(n, v)

            for odd in range(2):
                dve.sem_inc(s_out[odd], 1)
            sum_up(0, 0, 0)
            spread_of(0, 0)
            repeat(dve, finish, G, 2)
            last_sum(G - 1, (G - 1) // 2, (G - 1) % 2)

        @block.tensor
        def _(pe):

            def index_turn(half):
                pe.wait_ge(s_spread, half + 1)
                pe.matmul(ps_c[:, 0:16], spread[:, :, :].rearrange("p a b -> p (a b)"), cst[:, C_ROW16:C_ROW16 + 16],
                          start=True, stop=True).then_inc(s_idxps, 1)

            def turn(dst, src, done):
                for j in range(GT):
                    last = pe.transpose(dst[:, j * P:(j + 1) * P], src[:, j, :], ident)
                last.then_inc(done, 1)

            def scores(g, r):
                for t in (2 * r, 2 * r + 1):
                    for j in range(4):
                        last = pe.matmul(pscore[:, j, t % 2, :], kT[32 * j:32 * j + 32, t * P:(t + 1) * P],
                                         qeo[32 * j:32 * j + 32, t, :, :].rearrange("p i n -> p (i n)"),
                                         start=True, stop=True)
                last.then_inc(s_sc, 1)

            def retention(g, r):
                pe.wait_ge(s_prob, g * GT + 2 * r + 2)
                for t in (2 * r, 2 * r + 1):
                    for j in range(4):
                        for odd in range(2):
                            last = pe.matmul(ps_ret[32 * j:32 * j + 32, t * P:(t + 1) * P], vpad[:, t, odd, 32 * j:32 * j + 32],
                                             prob[:, t, 2 * j + odd, :], start=(odd == 0), stop=(odd == 1))
                if r == 1:
                    last.then_inc(s_ret, 1)

            def step(i):
                if here(i):
                    pe.wait_ge(s_kc, i + 1)
                    pe.wait_ge(s_qc, i * 2 + 2)
                    if here(i - 1):
                        pe.wait_ge(s_prob, i * GT)
                    scores(i, 0)
                if here(i - 3):
                    pe.wait_ge(s_xhat, i - 2)
                    if here(i):
                        pe.wait_ge(s_kc, i + 1)
                    turn(ps_b, xhat, s_t3)
                if here(i - 1):
                    retention(i - 1, 1)
                if here(i):
                    if here(i - 2):
                        pe.wait_ge(s_norm, i - 1)
                    for j in range(GT):
                        last = pe.matmul(ps_a[:, j * D:(j + 1) * D], lnT[:, j * P:(j + 1) * P], wvg[:, 0, :], start=True, stop=True)
                    last.then_inc(s_v, 1)
                if here(i - 3):
                    pe.wait_ge(s_xnT, i - 2)
                    if here(i - 1):
                        pe.wait_ge(s_retc, i)
                    if here(i - 4):
                        pe.wait_ge(s_rankc, (i - 3) * 2)
                    for j in range(GT):
                        last = pe.matmul(ps_ret[:, j * E:(j + 1) * E], xnTg[:, j * P:(j + 1) * P], wgate[:, :], start=True, stop=True)
                    last.then_inc(s_r, 1)
                if here(i):
                    if here(i - 3):
                        pe.wait_ge(s_xnT, i - 2)
                    pe.matmul(ps_b[:, :].rearrange("p (t d) -> p t d", t=GT), ones3[:, :],
                              bias_parts[:, E:E + 1, :].to_broadcast([3, GT, D]), start=True, stop=False)
                    for j in range(GT):
                        last = pe.matmul(ps_b[:, j * D:(j + 1) * D], lnT[:, j * P:(j + 1) * P], wvg[:, 1, :],
                                         start=False, stop=(j == GT - 1))
                    last.then_inc(s_g, 1)
                if here(i - 2):
                    pe.wait_ge(s_act, i - 1)
                    if here(i):
                        pe.wait_ge(s_qc, i * 2 + 2)
                    turn(ps_c, act_s, s_tz)
                if here(i - 1):
                    pe.wait_ge(s_retc, i)
                    if here(i):
                        pe.wait_ge(s_vc, i * 2 + 2)
                    turn(ps_a, retT, s_tret)
                if here(i + 1):
                    pe.wait_ge(s_ln, i + 2)
                    if here(i):
                        pe.wait_ge(s_gc, i + 1)
                    turn(ps_b, ln, s_t1)
                if here(i - 2):
                    pe.wait_ge(s_zT, i - 1)
                    for j in range(GT):
                        last = pe.matmul(ps_c[:, j * D:(j + 1) * D], actT[:, j * P:(j + 1) * P], wo_s[:, :], start=True, stop=True)
                    last.then_inc(s_wo, 1)
                if here(i - 3):
                    pe.wait_ge(s_pick, i - 2)
                    if here(i - 4):
                        pe.wait_ge(s_rankc, (i - 3) * 2)
                    seen = ps_ret[:, 0:GT * E].rearrange("p (t e) -> p t e", e=E)
                    pe.matmul(seen, earlier[:, :], chosen[:, :, :], start=True, stop=False)
                    for t in range(GT - 1):
                        pe.matmul(seen[:, t + 1:GT, :], ones[:, :], chosen[:, t:t + 1, :].to_broadcast([P, GT - 1 - t, E]),
                                  start=False, stop=False)
                    pe.matmul(seen, ones[:, :], before[:, :].unsqueeze(1).to_broadcast([P, GT, E]),
                              start=False, stop=True).then_inc(s_rank, 1)
                if here(i):
                    pe.wait_ge(s_prob, i * GT + 2)
                    scores(i, 1)
                if isinstance(i, int) and i == 1:
                    index_turn(1)
                if here(i + 1):
                    pe.wait_ge(s_lnT, i + 2)
                    pe.matmul(ps_b[:, :], wk_s[:, :], lnT[:, :], start=True, stop=True).then_inc(s_k, 1)
                    if isinstance(i, int) and i == 1:
                        pe.wait_ge(s_index, 2)
                    if here(i - 2):
                        pe.wait_ge(s_mixed, i - 1)
                    pe.matmul(ps_c[:, :], wq_s[:, :], lnT[:, :], start=True, stop=True).then_inc(s_q, 1)
                if here(i):
                    if here(i - 1):
                        pe.wait_ge(s_retc, i)
                    if here(i - 3):
                        pe.wait_ge(s_rankc, (i - 2) * 2 - 1)
                    pe.wait_ge(s_vc, i * 2 + 2)
                    retention(i, 0)

            pe.wait_ge(s_cst, 16)
            index_turn(0)
            pe.wait_ge(s_w, 16 * SMALL)
            pe.transpose(ps_a[:, 0:E * HC], b1_rows[:, :], ident[0:E * HC, 0:E * HC]).then_inc(s_b1t, 1)
            pe.wait_ge(s_b1, 1)
            pe.wait_ge(s_parts, 16)
            pe.wait_ge(s_prep, 4)
            pe.wait_ge(s_index, 1)
            mix_schedule(pe, step)
            pe.wait_ge(s_rankc, 2 * G)
            pe.matmul(ps_b[:, 0:E], ones[:, :], before[:, :], start=True, stop=True).then_inc(s_cnt, 1)
            pe.wait_ge(s_tab, 2)
            for k in range(2):
                last = pe.matmul(ps_c[0:1, k * P:(k + 1) * P], slot_cols[:, k:k + 1], ident, start=True, stop=True)
            last.then_inc(s_tab, 1)
            pe.wait_ge(s_wbig, 16 * 2 * E)
            pe.wait_ge(s_parts, 16)
            pe.wait_ge(s_tabT, 1)

            def turn_slot(n, i, u):
                pe.wait_ge(s_xin[u], (i + 1) * 16)
                if exists(n - 2, SLOTS):
                    pe.wait_ge(s_xTc, n - 1)
                pe.transpose(bank[u % 2][:, 0:P], xin[:, u, 0:D], ident).then_inc(s_xt, 1)

            def up(n, u):
                pe.wait_ge(s_xTc, n + 1)
                pe.wait_ge(s_w1, n + 1)
                if exists(n - 2, SLOTS):
                    pe.wait_ge(s_hid, (n - 1) * HC)
                for c in range(HC):
                    last = pe.matmul(bank[2 + u % 2][:, c * P:(c + 1) * P], w1_now[:, u % 2, c * P:(c + 1) * P], xT[:, u % 2, :],
                                     start=True, stop=True)
                last.then_inc(s_up, 1)

            def lower(n, u):
                e = pe.value_load(table[0:1, ds(n + P, 1)], min_val=0, max_val=E - 1)
                pe.wait_ge(s_hid, (n + 1) * HC)
                if exists(n - 2, SLOTS):
                    pe.wait_ge(s_y, n - 1)
                dst = down[u % 2][:, 0:D]
                pe.matmul(dst, ones3[:, :], bias_parts[:, ds(e, 1), :].rearrange("p a d -> p (a d)"), start=True, stop=False)
                for c in range(HC):
                    last = pe.matmul(dst, hid[:, u % 2, c, :], w2_s[:, ds(e, 1), c, :].rearrange("p a d -> p (a d)"),
                                     start=False, stop=(c == HC - 1))
                last.then_inc(s_down, 1)

            def slot(i, u):
                n, ni, v = ahead(i, u, 2, 4)
                if exists(n, SLOTS):
                    turn_slot(n, ni, v)
                n, ni, v = ahead(i, u, 1, 4)
                if exists(n, SLOTS):
                    up(n, v)
                lower(i * 4 + u, u)

            turn_slot(0, 0, 0)
            turn_slot(1, 0, 1)
            up(0, 0)
            repeat(pe, slot, SLOTS, 4)


_INS = ["x", "L0_tok_W", "L0_tok_b", "L0_attn_W_Q", "L0_attn_W_K", "L0_attn_W_V", "L0_attn_W_G", "L0_attn_W_O",
        "L0_attn_gn_weight", "L0_attn_gn_bias", "L0_ffn_Wg", "L0_ffn_W1", "L0_ffn_b1", "L0_ffn_W2", "L0_ffn_b2",
        "L0_ffn_ln_g", "L0_ffn_ln_b", "L0_ffn_out_g", "L0_ffn_out_b"]


def kernel(**inputs):
    import concourse.bacc as bacc
    from concourse.bass_utils import run_bass_kernel_spmd

    nc = bacc.Bacc("TRN2", target_bir_lowering=False, num_devices=1)
    arrays = {name: np.ascontiguousarray(inputs[name]) for name in _INS}
    arrays["consts"] = constants()
    args = [nc.dram_tensor(name, a.shape, mybir.dt.from_np(a.dtype), kind="ExternalInput").ap()
            for name, a in arrays.items()]
    out = nc.dram_tensor("out", (B, T, D), F32, kind="ExternalOutput").ap()
    routed = nc.dram_tensor("routed", (E * REGION + P, XW), F32, kind="Internal").ap()
    bias_rows = nc.dram_tensor("bias_rows", (3, E + 1, D), BF16, kind="Internal").ap()
    pairs = nc.dram_tensor("pairs", (PAIRS, D), F32, kind="Internal").ap()
    program(nc, *args, out, routed, pairs, bias_rows)
    return run_bass_kernel_spmd(nc, [arrays], core_ids=[0]).results[0]["out"]
```
